# Optimizing a Trainium2 kernel written in Bass

```python
import numpy as np
import jax
import jax.numpy as jnp

def _softmax(x, axis=-1):
    return jax.nn.softmax(x, axis=axis)

def _gelu(x):
    return jax.nn.gelu(x, approximate=True)

def _silu(x):
    return jax.nn.silu(x)

def _sigmoid(x):
    return jax.nn.sigmoid(x)

def _layernorm(x, axis=-1, eps=1e-05):
    m = jnp.mean(x, axis=axis, keepdims=True)
    v = jnp.var(x, axis=axis, keepdims=True)
    return (x - m) / jnp.sqrt(v + eps)

def _scatter_add(tgt, idx, src, axis=0):
    return tgt.at[idx].add(src)

def _segment_sum(src, seg, n):
    return jax.ops.segment_sum(src, seg, n)
kernel_name = 'mk_gnn_resnorm_d1_gnn_r32_639589'

def setup_inputs(seed: int=0):
    np.random.seed(seed)
    _w = jnp.asarray

    def _rec_inputs():
        import jax
        import jax.numpy as jnp
        _gk = jax.random.key(seed)
        x = -0.0003713 + 1 * jax.random.normal(jax.random.fold_in(_gk, 1), (50000, 128), jnp.float32)
        src = jax.random.randint(jax.random.fold_in(_gk, 2), (25000,), 0, 50000, jnp.int32)
        dst = jax.random.randint(jax.random.fold_in(_gk, 3), (25000,), 0, 50000, jnp.int32)
        _o = jnp.argsort(dst, stable=True)
        src = src[_o]
        dst = dst[_o]
        edge_attr_128 = -6.47781e-05 + 0.999943 * jax.random.normal(jax.random.fold_in(_gk, 12), (25000, 128), jnp.float32)
        return (x, src, dst, edge_attr_128)
    x, src, dst, edge_attr_128 = _rec_inputs()

    def _L0_gnn_setup():
        import jax, jax.numpy as jnp
        import numpy as np
        N, E, G, DIM = (3125, 50000, 64, 128)
        BN_EPS = 1e-05

        def _bn(h, gamma, beta):
            mu = jnp.mean(h, axis=0)
            var = jnp.var(h, axis=0)
            return (h - mu) * jax.lax.rsqrt(var + BN_EPS) * gamma + beta
        key = jax.random.key(seed)
        ks = jax.random.split(key, 20)
        inp = {'x': jax.random.normal(ks[0], (N, DIM), jnp.float32), 'edge_attr': jax.random.normal(ks[1], (E, DIM), jnp.float32), 'u': jax.random.normal(ks[2], (G, DIM), jnp.float32), 'edge_index': jax.random.randint(ks[3], (2, E), 0, N, jnp.int32), 'batch': jnp.sort(jax.random.randint(ks[4], (N,), 0, G, jnp.int32))}

        def xavier(k, shape):
            fan_in, fan_out = (shape[1], shape[0])
            lim = jnp.sqrt(6.0 / (fan_in + fan_out))
            return jax.random.uniform(k, shape, jnp.float32, -lim, lim)
        inp['W0'] = xavier(ks[5], (DIM, 3 * DIM))
        inp['b0'] = jnp.zeros((DIM,), jnp.float32)
        inp['W1'] = xavier(ks[6], (DIM, DIM))
        inp['b1'] = jnp.zeros((DIM,), jnp.float32)
        inp['W2'] = xavier(ks[7], (DIM, DIM))
        inp['b2'] = jnp.zeros((DIM,), jnp.float32)
        for i in range(3):
            inp[f'g{i}'] = jnp.ones((DIM,), jnp.float32)
            inp[f'bt{i}'] = jnp.zeros((DIM,), jnp.float32)
        return inp
    _L0_gnn_all = _L0_gnn_setup()
    _L0_gnn_in = {k: v for k, v in _L0_gnn_all.items() if k in ('u', 'W0', 'b0', 'W1', 'b1', 'W2', 'b2', 'g0', 'bt0', 'g1', 'bt1', 'g2', 'bt2')}
    del _L0_gnn_all
    return {'x': x, 'src': src, 'dst': dst, 'edge_attr_128': edge_attr_128, 'L0_gnn_u': _L0_gnn_in['u'], 'L0_gnn_W0': _L0_gnn_in['W0'], 'L0_gnn_b0': _L0_gnn_in['b0'], 'L0_gnn_W1': _L0_gnn_in['W1'], 'L0_gnn_b1': _L0_gnn_in['b1'], 'L0_gnn_W2': _L0_gnn_in['W2'], 'L0_gnn_b2': _L0_gnn_in['b2'], 'L0_gnn_g0': _L0_gnn_in['g0'], 'L0_gnn_bt0': _L0_gnn_in['bt0'], 'L0_gnn_g1': _L0_gnn_in['g1'], 'L0_gnn_bt1': _L0_gnn_in['bt1'], 'L0_gnn_g2': _L0_gnn_in['g2'], 'L0_gnn_bt2': _L0_gnn_in['bt2']}

def reference(x, src, dst, edge_attr_128, L0_gnn_u, L0_gnn_W0, L0_gnn_b0, L0_gnn_W1, L0_gnn_b1, L0_gnn_W2, L0_gnn_b2, L0_gnn_g0, L0_gnn_bt0, L0_gnn_g1, L0_gnn_bt1, L0_gnn_g2, L0_gnn_bt2):
    import jax
    import jax.numpy as jnp

    def _L0_gnn_ref(x, edge_attr, u, W0, b0, W1, b1, W2, b2, g0, bt0, g1, bt1, g2, bt2, edge_index, batch):
        import jax, jax.numpy as jnp
        import numpy as np
        N, E, G, DIM = (3125, 50000, 64, 128)
        BN_EPS = 1e-05

        def _bn(h, gamma, beta):
            mu = jnp.mean(h, axis=0)
            var = jnp.var(h, axis=0)
            return (h - mu) * jax.lax.rsqrt(var + BN_EPS) * gamma + beta
        n = x.shape[0]
        src = edge_index[0]
        sums = jax.ops.segment_sum(edge_attr, src, num_segments=n)
        cnt = jax.ops.segment_sum(jnp.ones((edge_attr.shape[0],), edge_attr.dtype), src, num_segments=n)
        v_e = sums / jnp.maximum(cnt, 1.0)[:, None]
        out = jnp.concatenate([x, v_e, u[batch]], axis=1)
        for W, b, g, bt in ((W0, b0, g0, bt0), (W1, b1, g1, bt1), (W2, b2, g2, bt2)):
            out = jax.nn.relu(out @ W.T + b)
            out = _bn(out, g, bt)
        return out
    edge_index = jnp.stack([src, dst])
    batch0 = jnp.zeros((50000,), jnp.int32)
    x = _layernorm(x + _L0_gnn_ref(x, edge_attr_128, L0_gnn_u, L0_gnn_W0, L0_gnn_b0, L0_gnn_W1, L0_gnn_b1, L0_gnn_W2, L0_gnn_b2, L0_gnn_g0, L0_gnn_bt0, L0_gnn_g1, L0_gnn_bt1, L0_gnn_g2, L0_gnn_bt2, edge_index, batch0), axis=-1)
    return x

_drawn_inputs = setup_inputs


def setup_inputs(seed=0):
    import zlib

    import numpy as np

    out = dict(_drawn_inputs(seed))
    spreads = {'L0_gnn_b0': (0.0, 0.1),
     'L0_gnn_b1': (0.0, 0.1),
     'L0_gnn_b2': (0.0, 0.1),
     'L0_gnn_g0': (1.0, 0.2),
     'L0_gnn_bt0': (0.0, 0.1),
     'L0_gnn_g1': (1.0, 0.2),
     'L0_gnn_bt1': (0.0, 0.1),
     'L0_gnn_g2': (1.0, 0.2),
     'L0_gnn_bt2': (0.0, 0.1)}
    factors = {}
    for name, (base, spread) in spreads.items():
        noise = np.random.default_rng([zlib.crc32(name.encode()), seed]).standard_normal(out[name].shape)
        drawn = base * np.exp(spread * noise) if base else spread * noise
        out[name] = jnp.asarray(drawn.astype(out[name].dtype))
    for name, factor in factors.items():
        out[name] = (out[name] * factor).astype(out[name].dtype)
    return out
```

```python
import concourse.bass as bass
from concourse import mybir
from contextlib import ExitStack


def gnn_resnorm_kernel(nc, x, src, edge_attr, u, W0, b0, W1, b1, W2, b2, g0, bt0, g1, bt1, g2, bt2, table, out):
    fp32, bf16, fp16, i32 = mybir.dt.float32, mybir.dt.bfloat16, mybir.dt.float16, mybir.dt.int32
    ALU = mybir.AluOpType
    ACT = mybir.ActivationFunctionType
    AX = mybir.AxisListType.X

    N, D = x.shape
    E = edge_attr.shape[0]
    P = 128
    BI = 8
    BN = P * BI
    NBF = N // BN
    PL = (N - NBF * BN) // BI
    NB = NBF + 1
    NT = NB * BI
    HT = 4
    HC = HT * P
    NH = 2 * NB
    NHF = 2 * NBF
    EBF = E // BN
    ET = EBF * BI
    EPL = (E - EBF * BN) // BI
    EB = EBF + 1
    NE = EB * BI
    RW = D + 1
    SLOTS = P * NT
    ZT = 14
    NZ = NT // ZT
    EPS = 1e-5
    PER = 4
    assert N % BI == 0 and E % BI == 0 and NT % ZT == 0 and NHF % PER == 0 and 0 < PL < P and 0 < EPL < P

    x_full = x[0:NBF * BN, :].rearrange("(g p s i) f -> p s g (i f)", p=P, s=2, i=HT)
    x_last = x[NBF * BN:N, :].rearrange("(p s i) f -> p s (i f)", s=2, i=HT)
    o_full = out[0:NBF * BN, :].rearrange("(g p s i) f -> p s g (i f)", p=P, s=2, i=HT)
    o_last = out[NBF * BN:N, :].rearrange("(p s i) f -> p s (i f)", s=2, i=HT)
    e_full = edge_attr[0:EBF * BN, :].rearrange("(p t) f -> p (t f)", p=P)
    e_last = edge_attr[EBF * BN:E, :].rearrange("(p t) f -> p (t f)", t=BI)
    src_full = src[0:EBF * BN].rearrange("(p t) -> p t", p=P)
    src_last = src[EBF * BN:E].rearrange("(p t) -> p t", t=BI)
    tab = table[0:SLOTS, :].rearrange("(p j) c -> p (j c)", p=P)

    ctx = ExitStack()
    with ctx:
        def sb(name, shape, dt=fp32, where=ctx):
            return where.enter_context(nc.sbuf_tensor(name, shape, dt))

        def sem(name):
            return ctx.enter_context(nc.semaphore(name))

        ident = sb("ident", [P, P])
        lo1_row = sb("lo1_row", [P, P])
        W0aT = sb("W0aT", [P, P])
        W1T = sb("W1T", [P, P])
        W2T = sb("W2T", [P, P])
        vecs = sb("vecs", [P, 10])
        rcnt = sb("rcnt", [P, NT])
        stats = sb("stats", [P, NH, 6])
        agg = sb("agg", [P, 2])
        bn_std = sb("bn_std", [P, 1])
        bn_a = sb("bn_a", [P, 3])
        bn_c = sb("bn_c", [P, 3])
        bn_t = sb("bn_t", [P, 1])
        bias = sb("bias", [P, 3])
        ovf = sb("ovf", [P, 1], i32)
        xr = sb("xr", [P, 4, HC])
        tabr = sb("tabr", [P, 2, BI * RW])
        stage = sb("stage", [P, 2, HC])
        oneh = sb("oneh", [P, 2, 2, P])
        lnst = sb("lnst", [P, 2, HT, 6])
        lnm = sb("lnm", [P, 8, HT])
        h_last = tabr[:, 1, 0:BI * PL]

        ps = ctx.enter_context(nc.psum_tensor("ps", [P, 8, 512], fp32))

        sa = ExitStack()
        with sa:
            rows = sb("rows", [P, NE, RW], where=sa)
            er = sb("er", [P, 4, BI * D], where=sa)
            eT = sb("eT", [P, 2, 512], where=sa)
            hi_row = sb("hi_row", [P, NT], fp16, sa)
            iot = sb("iot", [P, NT], i32, sa)
            pidx_i = sb("pidx_i", [P, 1], i32, sa)
            pidx = sb("pidx", [P, 1], fp32, sa)
            lo_row = sb("lo_row", [P, P], fp16, sa)
            ohh = sb("ohh", [P, 4, NT], bf16, sa)
            ohl = sb("ohl", [P, 4, P], bf16, sa)
            junk = sb("junk", [P, 2, NT], bf16, sa)
            before = sb("before", [P, P], bf16, sa)
            notbefore = sb("notbefore", [P, P], bf16, sa)
            srcI = sb("srcI", [P, NE], i32, sa)
            t1 = sb("t1", [P, NE], i32, sa)
            t2 = sb("t2", [P, NE], i32, sa)
            t3 = sb("t3", [P, NE], i32, sa)
            hiF = sb("hiF", [P, NE], fp32, sa)
            loF = sb("loF", [P, NE], fp32, sa)
            rank = sb("rank", [P, BI], fp32, sa)
            slot0 = sb("slot0", [P, NE], fp32, sa)
            dump_i = sb("dump_i", [P, NE], i32, sa)
            dump = sb("dump", [P, NE], fp32, sa)
            posf = sb("posf", [P, 4, BI], fp32, sa)
            posI = sb("posI", [P, NE], i32, sa)
            zero = sb("zero", [P, ZT * RW], fp32, sa)
            wraw = sb("wraw", [P, 5, P], fp32, sa)
            vraw = sb("vraw", [10, P], fp32, sa)
            W0bT = sb("W0bT", [P, P], fp32, sa)
            W0cT = sb("W0cT", [P, P], fp32, sa)
            tot = sb("tot", [P, NT], fp32, sa)
            tmax = sb("tmax", [P, 1], fp32, sa)
            f_e = sb("f_e", [P, D], fp32, sa)
            f_eT = sb("f_eT", [P, P], fp32, sa)
            f_p = sb("f_p", [P, D], fp32, sa)
            f_key = sb("f_key", [P, 4], fp32, sa)
            f_get = sb("f_get", [P, 1], i32, sa)
            f_put = sb("f_put", [P, 1], i32, sa)
            f_kb = sb("f_kb", [P, P], fp32, sa)
            f_same = sb("f_same", [P, P], fp32, sa)
            f_earlier = sb("f_earlier", [P, P], fp32, sa)
            f_junk = sb("f_junk", [P, P], fp32, sa)
            f_old = sb("f_old", [P, RW], fp32, sa)
            f_new = sb("f_new", [P, RW], fp32, sa)
        h = sb("h", [P, NHF * HC])

        w_in, v_in, src_in, zero_done, scat_done = (
            sem("w_in"), sem("v_in"), sem("src_in"), sem("zero_done"), sem("scat_done"))
        e_in = [sem(f"e_in{i}") for i in range(4)]
        x_in = [sem(f"x_in{i}") for i in range(4)]
        x2_in = [sem(f"x2_in{i}") for i in range(4)]
        tab_in = [sem(f"tab_in{i}") for i in range(2)]
        out_w = [sem(f"out_w{i}") for i in range(4)]
        iota_ok, zero_ok, const_ok, srcset, meta_ok = (
            sem("iota_ok"), sem("zero_ok"), sem("const_ok"), sem("srcset"), sem("meta_ok"))
        wT_done, wT_ready, b0_done, bias_ok = sem("wT_done"), sem("wT_ready"), sem("b0_done"), sem("bias_ok")
        oh_ready, tri_done, rank_ready, cmp_done, pos_ready = (
            sem("oh_ready"), sem("tri_done"), sem("rank_ready"), sem("cmp_done"), sem("pos_ready"))
        eT_done, eT_ready, pj_done, rows_ready = sem("eT_done"), sem("eT_ready"), sem("pj_done"), sem("rows_ready")
        dve_s, ovf_ok, rcnt_ok = sem("dve_s"), sem("ovf_ok"), sem("rcnt_ok")
        turn = sem("turn")
        xT_done, xT_ready, mx_done, oh0_ready, mz_done, zs, sum_ready, hT_done, h0_ready, st0 = (
            sem("xT_done"), sem("xT_ready"), sem("mx_done"), sem("oh0_ready"), sem("mz_done"), sem("zs"),
            sem("sum_ready"), sem("hT_done"), sem("h0_ready"), sem("st0"))
        f_zero, f_in, f_got, f_done = sem("f_zero"), sem("f_in"), sem("f_got"), sem("f_done")
        f_T, f_Tc, f_P, f_Pc, f_keys, f_row, f_idx, f_C, f_sum, fch = (
            sem("f_T"), sem("f_Tc"), sem("f_P"), sem("f_Pc"), sem("f_keys"), sem("f_row"), sem("f_idx"), sem("f_C"),
            sem("f_sum"), sem("fch"))
        f_sameok = sem("f_sameok")
        mm = [None, sem("mm1"), sem("mm2")]
        hr = [None, sem("hr1"), sem("hr2")]
        stl = [st0, sem("st1"), sem("st2")]
        agg_ok, std_ok, fold_ok, bmm_ok, ac_ok, bch = (
            sem("agg_ok"), sem("std_ok"), sem("fold_ok"), sem("bmm_ok"), sem("ac_ok"), sem("bch"))
        y_ready, yT_done, res_ready, lnst_ok, lnv_ok, lnsd_ok, lnr_ok, ln_ready, lch = (
            sem("y_ready"), sem("yT_done"), sem("res_ready"), sem("lnst_ok"), sem("lnv_ok"), sem("lnsd_ok"),
            sem("lnr_ok"), sem("ln_ready"), sem("lch"))

        def wait(eng, s, n):
            if not (isinstance(n, int) and n <= 0):
                eng.wait_ge(s, n)

        def np_(q):
            return PL if isinstance(q, int) and q >= NHF else P

        def hcol(q):
            if isinstance(q, int) and q >= NHF:
                return h_last[:, (q - NHF) * HT * PL:(q - NHF + 1) * HT * PL]
            return h[:, bass.ds(q * HC, HC)] if not isinstance(q, int) else h[:, q * HC:(q + 1) * HC]

        def halves(eng, step):
            for q in range(PER):
                step(q, q)
            with eng.Fori(1, NHF // PER - 1) as it:
                for s in range(PER):
                    step(it * PER + s, s)
            for q in range(NHF - PER, NH):
                step(q, q % PER)

        def edge_blocks(eng, step):
            step(0)
            with eng.Fori(1, EBF) as b:
                step(b)
            step(EBF)

        def ep(b):
            return EPL if isinstance(b, int) and b == EBF else P

        def rebuild(eng, step):
            eng.wait_ge(ovf_ok, 1)
            full = eng.value_load(ovf[0:1, 0:1], min_val=0, max_val=1)
            with eng.If(full):
                with eng.Fori(0, ET) as t:
                    step(t, P)
                for t in range(ET, NE):
                    step(t, EPL)
                eng.wait_ge(f_done, 16 * NE)

        block = ctx.enter_context(nc.Block())

        @block.sync
        def _(sp):
            sp.wait_ge(srcset, 1)
            sp.dma_start(srcI[:, 0:ET], src_full).then_inc(src_in, 16)
            sp.dma_start(srcI[0:EPL, ET:NE], src_last).then_inc(src_in, 16)
            sp.dma_start(wraw[:, 0:3, :].rearrange("p a b -> p (a b)"), W0).then_inc(w_in, 16)
            sp.dma_start(wraw[:, 3, :], W1).then_inc(w_in, 16)
            sp.dma_start(wraw[:, 4, :], W2).then_inc(w_in, 16)
            for k, v in enumerate((None, b0, b1, b2, g0, bt0, g1, bt1, g2, bt2)):
                sp.dma_start(vraw[k:k + 1, :], u[0:1, :] if k == 0 else v.rearrange("(a b) -> a b", a=1)).then_inc(v_in, 16)

            def load_edges(b, r):
                wait(sp, eT_done, 2 * (b - 3))
                if isinstance(b, int) and b == EBF:
                    sp.dma_start(er[0:EPL, r, :], e_last).then_inc(e_in[r], 16)
                else:
                    cols = (slice(b * BN, (b + 1) * BN) if isinstance(b, int) else bass.ds(b * BN, BN))
                    sp.dma_start(er[:, r, :], e_full[:, cols]).then_inc(e_in[r], 16)

            for b in range(4):
                load_edges(b, b)
            with sp.Fori(1, EBF // 4) as it:
                for r in range(4):
                    load_edges(it * 4 + r, r)
            for b in range(EBF // 4 * 4, EB):
                load_edges(b, b % 4)

            def load_x(q, s):
                wait(sp, hT_done, q - 3)
                if isinstance(q, int) and q >= NHF:
                    sp.dma_start(xr[0:PL, s, :], x_last[:, q % 2, :]).then_inc(x_in[s], 16)
                else:
                    g = q // 2 if isinstance(q, int) else None
                    sp.dma_start(xr[:, s, :], x_full[:, s % 2, g, :]).then_inc(x_in[s], 16)

            def load_x_dyn(it, s):
                q = it * PER + s
                wait(sp, hT_done, q - 3)
                sp.dma_start(xr[:, s, :], x_full[:, s % 2, bass.ds(it * 2 + s // 2, 1), :]).then_inc(x_in[s], 16)

            def load_table(g, r):
                wait(sp, mz_done, 4 * (g - 1))
                cols = (slice(g * BI * RW, (g + 1) * BI * RW) if isinstance(g, int) else bass.ds(g * (BI * RW), BI * RW))
                sp.dma_start(tabr[:, r, :], tab[:, cols]).then_inc(tab_in[r], 16)

            for q in range(PER):
                load_x(q, q)
            sp.wait_ge(scat_done, 16 * NE)

            def fetch(t, p):
                wait(sp, f_done, 16 * t)
                v = e_last[:, (t - ET) * D:(t - ET + 1) * D] if isinstance(t, int) else e_full[:, bass.ds(t * D, D)]
                sp.dma_start(f_e[0:p, :], v).then_inc(f_in, 16)

            rebuild(sp, fetch)
            load_table(0, 0)
            load_table(1, 1)
            with sp.Fori(1, NHF // PER) as it:
                for s in range(PER):
                    load_x_dyn(it, s)
                    if s % 2:
                        load_table(it * 2 + s // 2, s // 2)
            for q in range(NHF, NH):
                load_x(q, q % PER)
            load_table(NBF, 0)

            def load_x2(q, s, xv):
                wait(sp, out_w[s], 16 * ((q - s) // PER) if isinstance(q, int) else 16 * xv)
                if isinstance(q, int):
                    v = x_last[:, q % 2, :] if q >= NHF else x_full[:, s % 2, q // 2, :]
                    sp.dma_start(xr[0:np_(q), s, :], v).then_inc(x2_in[s], 16)
                else:
                    sp.dma_start(xr[:, s, :], x_full[:, s % 2, bass.ds(xv * 2 + s // 2, 1), :]).then_inc(x2_in[s], 16)

            def store(q, s, xv):
                sp.wait_ge(ln_ready, q + 1)
                if isinstance(q, int):
                    v = o_last[:, q % 2, :] if q >= NHF else o_full[:, s % 2, q // 2, :]
                    sp.dma_start(v, xr[0:np_(q), s, :]).then_inc(out_w[s], 16)
                else:
                    sp.dma_start(o_full[:, s % 2, bass.ds(xv * 2 + s // 2, 1), :], xr[:, s, :]).then_inc(out_w[s], 16)

            sp.wait_ge(hT_done, NH)
            for q in range(PER):
                load_x2(q, q, None)
            for s in range(2):
                store(s, s, None)
            with sp.Fori(1, NHF // PER) as it:
                for s in range(PER):
                    if s < 2:
                        store_q = it * PER + s - 2
                        sp.wait_ge(ln_ready, store_q + 1)
                        sp.dma_start(o_full[:, s % 2, bass.ds(it * 2 - 1, 1), :], xr[:, s + 2, :]).then_inc(out_w[s + 2], 16)
                    else:
                        store(it * PER + s - 2, s - 2, it)
                    load_x2(it * PER + s, s, it)
            for q in range(NHF, NH):
                store(q - 2, (q - 2) % PER, None)
                load_x2(q, q % PER, None)
            for q in range(NH - 2, NH):
                store(q, q % PER, None)
            for s in range(PER):
                sp.wait_ge(out_w[s], 16 * len(range(s, NH, PER)))

        @block.gpsimd
        def _(pool):
            nc.gpsimd.memset(srcI[:, ET:NE], 0).then_inc(srcset, 1)
            nc.gpsimd.memset(zero[:], 0.0).then_inc(zero_ok, 1)
            nc.gpsimd.iota(iot[:], [[1, NT]], base=0, channel_multiplier=0).then_inc(iota_ok, 1)
            nc.gpsimd.iota(pidx_i[:], [[0, 1]], base=0, channel_multiplier=1).then_inc(iota_ok, 1)
            nc.gpsimd.iota(dump_i[:], [[P, NE]], base=SLOTS, channel_multiplier=1).then_inc(iota_ok, 1)
            pool.wait_ge(zero_ok, 1)
            for z in range(NZ):
                pool.dma_start(tab[:, z * ZT * RW:(z + 1) * ZT * RW], zero[:]).then_inc(zero_done, 16)
            pool.wait_ge(zero_done, 16 * NZ)

            for b in range(EB):
                pool.wait_ge(pos_ready, b + 1)
                pool.wait_ge(rows_ready, 2 * (b + 1))
                p = ep(b)
                for t in range(b * BI, (b + 1) * BI):
                    pool.indirect_dma_start(
                        out=table[:, :], out_offset=bass.IndirectOffsetOnAxis(ap=posI[0:p, t:t + 1], axis=0),
                        in_=rows[0:p, t, :], in_offset=None).then_inc(scat_done, 16)

            def gather_scatter(t, p):
                pool.wait_ge(f_zero, 16 * NZ)
                wait(pool, f_done, 16 * t)
                pool.wait_ge(f_idx, t + 1)
                pool.sem_inc(turn, 1)
                pool.indirect_dma_start(out=f_old[0:p, :], out_offset=None, in_=table[0:SLOTS, :],
                                        in_offset=bass.IndirectOffsetOnAxis(ap=f_get[0:p, 0:1], axis=0)).then_inc(f_got, 16)
                pool.wait_ge(f_sum, t + 1)
                pool.sem_inc(turn, 1)
                pool.indirect_dma_start(out=table[:, :], out_offset=bass.IndirectOffsetOnAxis(ap=f_put[0:p, 0:1], axis=0),
                                        in_=f_new[0:p, :], in_offset=None).then_inc(f_done, 16)

            pool.wait_ge(ovf_ok, 1)
            with pool.If(pool.value_load(ovf[0:1, 0:1], min_val=0, max_val=1)):
                pool.wait_ge(scat_done, 16 * NE)
                for z in range(NZ):
                    pool.dma_start(tab[:, z * ZT * RW:(z + 1) * ZT * RW], zero[:]).then_inc(f_zero, 16)
            rebuild(pool, gather_scatter)

            def onehots(q, s):
                g2 = s // 2
                pool.wait_ge(tab_in[g2], 16 * (q // PER + 1) if isinstance(q, int) else 16 * ((q - s) // PER + 1))
                pn = np_(q)
                for k in range(2):
                    wait(pool, mz_done, 2 * q + k - 1)
                    pool.sem_inc(turn, 1)
                    for j in range(2):
                        i = (s % 2) * HT + 2 * k + j
                        last = nc.gpsimd.tensor_scalar(oneh[:, k, j, 0:pn], lo1_row[:, 0:pn],
                                                       tabr[:, g2, i * RW + D:i * RW + D + 1], None, ALU.is_equal)
                    last.then_inc(oh0_ready, 1)

            halves(pool, onehots)

            def apply_ln(q, s):
                pool.wait_ge(lnr_ok, q + 1)
                pool.sem_inc(turn, 1)
                pn = np_(q)
                for j in range(HT):
                    v = xr[0:pn, s, j * D:(j + 1) * D]
                    last = nc.gpsimd.tensor_scalar(v, v, lnm[0:pn, 4 * (s % 2), j:j + 1], lnm[0:pn, 4 * (s % 2) + 3, j:j + 1],
                                                   ALU.subtract, ALU.mult)
                last.then_inc(ln_ready, 1)

            halves(pool, apply_ln)

        @block.scalar
        def _(act):
            def project(b):
                for k in range(2):
                    hf = 2 * b + k
                    p = ep(b)
                    act.wait_ge(eT_done, hf + 1)
                    wait(act, pj_done, hf - 1)
                    nc.scalar.activation(eT[:, k, :].rearrange("f (i e) -> f i e", i=HT)[:, :, 0:p],
                                         ps[:, 3 + k, :].rearrange("f (i e) -> f i e", i=HT)[:, :, 0:p],
                                         ACT.Copy).then_inc(eT_ready, 1)
                    act.wait_ge(pj_done, hf + 1)
                    t = hf * HT
                    dst = rows[0:p, t:t + HT, 0:D] if isinstance(t, int) else rows[:, bass.ds(t, HT), 0:D]
                    nc.scalar.activation(dst, ps[0:p, 5 + k, :].rearrange("e (i f) -> e i f", i=HT),
                                         ACT.Copy).then_inc(rows_ready, 1)

            edge_blocks(act, project)

            def copies(t, p):
                act.wait_ge(f_T, t + 1)
                nc.scalar.activation(f_eT[:, 0:p], ps[:, 3, 0:p], ACT.Copy).then_inc(f_Tc, 1)
                act.wait_ge(f_P, t + 1)
                nc.scalar.activation(f_p[0:p, :], ps[0:p, 5, 0:D], ACT.Copy).then_inc(f_Pc, 1)

            rebuild(act, copies)

            def copy_xT(q, s):
                act.wait_ge(xT_done, q + 1)
                wait(act, mx_done, q - 1)
                pn = np_(q)
                nc.scalar.activation(stage[:, s % 2, :].rearrange("f (i e) -> f i e", i=HT)[:, :, 0:pn],
                                     ps[:, s % 2, :].rearrange("f (i e) -> f i e", i=HT)[:, :, 0:pn],
                                     ACT.Copy).then_inc(xT_ready, 1)

            def relu0(q, s):
                act.wait_ge(hT_done, q + 1)
                pn = np_(q)
                nc.scalar.activation(hcol(q), ps[:, 6 + s % 2, 0:HT * pn], ACT.Relu, bias=bias[:, 0:1]).then_inc(h0_ready, 1)

            act.wait_ge(bias_ok, 1)
            copy_xT(0, 0)

            def layer0(q, s):
                if not (isinstance(q, int) and q == NH - 1):
                    copy_xT(q + 1, (s + 1) % PER)
                if not (isinstance(q, int) and q == 0):
                    relu0(q - 1, (s - 1) % PER)

            halves(act, layer0)
            relu0(NH - 1, (NH - 1) % PER)

            def bn_sqrt(l):
                act.wait_ge(agg_ok, l + 1)
                nc.scalar.activation(bn_std[:], bn_t[:], ACT.Sqrt).then_inc(std_ok, 1)

            bn_sqrt(0)
            for l in (1, 2):
                act.wait_ge(fold_ok, l)

                def layer(q, s):
                    act.wait_ge(mm[l], q + 1)
                    pn = np_(q)
                    nc.scalar.activation(hcol(q), ps[:, s, 0:HT * pn], ACT.Relu, bias=bias[:, l:l + 1]).then_inc(hr[l], 1)

                halves(act, layer)
                bn_sqrt(l)

            act.wait_ge(ac_ok, 3)

            def normalise(q, s):
                wait(act, yT_done, q - 1)
                pn = np_(q)
                nc.scalar.activation(stage[:, s % 2, 0:HT * pn], hcol(q), ACT.Identity,
                                     bias=bn_c[:, 2:3], scale=bn_a[:, 2:3]).then_inc(y_ready, 1)

            def ln_sqrt(q, s):
                act.wait_ge(lnv_ok, q + 1)
                pn = np_(q)
                nc.scalar.activation(lnm[0:pn, 4 * (s % 2) + 2, :], lnm[0:pn, 4 * (s % 2) + 1, :], ACT.Sqrt).then_inc(lnsd_ok, 1)

            normalise(0, 0)

            def final(q, s):
                if not (isinstance(q, int) and q == NH - 1):
                    normalise(q + 1, (s + 1) % PER)
                if not (isinstance(q, int) and q == 0):
                    ln_sqrt(q - 1, (s - 1) % PER)

            halves(act, final)
            ln_sqrt(NH - 1, (NH - 1) % PER)

        @block.vector
        def _(dve):
            chain = [0]

            def link(ins):
                chain[0] += 1
                ins.then_inc(dve_s, 1)
                dve.wait_ge(dve_s, chain[0])

            dve.wait_ge(iota_ok, 3)
            nc.vector.tensor_copy(hi_row[:], iot[:])
            nc.vector.tensor_copy(lo_row[:], iot[:, 0:P])
            nc.vector.tensor_scalar(lo1_row[:], iot[:, 0:P], 1.0, None, ALU.add)
            link(nc.vector.tensor_copy(pidx[:], pidx_i[:]))
            nc.vector.tensor_scalar(ident[:], lo_row[:], pidx[:, 0:1], None, ALU.is_equal)
            nc.vector.tensor_scalar(before[:], lo_row[:], pidx[:, 0:1], None, ALU.is_gt)
            nc.vector.tensor_scalar(notbefore[:], lo_row[:], pidx[:, 0:1], None, ALU.is_le)
            nc.vector.tensor_scalar(f_earlier[:], lo_row[:], pidx[:, 0:1], None, ALU.is_lt)
            nc.vector.tensor_copy(dump[:], dump_i[:]).then_inc(const_ok, 1)

            dve.wait_ge(src_in, 32)
            nc.vector.tensor_scalar(t1[:], srcI[:], 7, 0x1FFFFF8, ALU.logical_shift_right, ALU.bitwise_and)
            nc.vector.tensor_scalar(t2[:], srcI[:], 7, None, ALU.bitwise_and)
            link(nc.vector.tensor_scalar(t3[:], srcI[:], 3, 127, ALU.logical_shift_right, ALU.bitwise_and))
            nc.vector.tensor_copy(loF[:], t3[:])
            link(nc.vector.tensor_tensor(hiF[:], t1[:], t2[:], ALU.add))
            nc.vector.tensor_scalar(slot0[:].rearrange("p (a b) -> p a b", b=2)[:, :, 1],
                                    hiF[:].rearrange("p (a b) -> p a b", b=2)[:, :, 1], float(P // 2 * NT), None, ALU.add)
            nc.vector.tensor_copy(slot0[:].rearrange("p (a b) -> p a b", b=2)[:, :, 0],
                                  hiF[:].rearrange("p (a b) -> p a b", b=2)[:, :, 0])
            nc.vector.tensor_scalar(rows[:, :, D:D + 1].rearrange("p t a -> p (t a)"), loF[:], 1.0, None,
                                    ALU.add).then_inc(meta_ok, 1)
            dve.wait_ge(meta_ok, 1)

            dve.wait_ge(wT_done, 1)
            for dst, bank, k in ((W0aT, 0, 0), (W0bT, 0, 1), (W0cT, 0, 2), (W1T, 0, 3), (W2T, 1, 0)):
                nc.vector.tensor_copy(dst[:], ps[:, bank, k * P:(k + 1) * P])
            nc.vector.tensor_copy(vecs[:], ps[:, 1, P:P + 10]).then_inc(wT_ready, 1)
            dve.wait_ge(b0_done, 1)
            dve.wait_ge(wT_ready, 1)
            nc.vector.tensor_tensor(bias[:, 0:1], ps[:, 2, 0:1], vecs[:, 1:2], ALU.add).then_inc(bias_ok, 1)

            def onehot(t, i, p):
                wait(dve, cmp_done, t - 3)
                r = i % 4
                sc = (lambda a: a[0:p, t:t + 1]) if isinstance(t, int) else (lambda a: a[:, bass.ds(t, 1)])
                nc.vector.tensor_scalar(ohh[0:p, r, :], hi_row[0:p, :], sc(hiF), None, ALU.is_equal)
                nc.vector.tensor_scalar(ohl[0:p, r, :], lo_row[0:p, :], sc(loF), None, ALU.is_equal).then_inc(oh_ready, 1)

            def select(t, i, p):
                dve.wait_ge(tri_done, t + 1)
                nc.vector.tensor_tensor_reduce(out=junk[0:p, i % 2, :], in0=ohh[0:p, i % 4, :], in1=ps[0:p, i % 2, 0:NT],
                                               scale=1.0, scalar=0.0, op0=ALU.mult, op1=ALU.add,
                                               accum_out=rank[0:p, i:i + 1]).then_inc(rank_ready, 1)

            link(nc.vector.memset(rank[:], 0.0))
            onehot(0, 0, P)
            c0 = chain[0]

            def slots(b):
                p, pn = ep(b), ep(b + 1 if isinstance(b, int) else b)
                for i in range(BI):
                    t = b * BI + i
                    if not (isinstance(t, int) and t == NE - 1):
                        onehot(t + 1, (i + 1) % BI, pn if i == BI - 1 else p)
                    select(t, i, p)
                dve.wait_ge(rank_ready, (b + 1) * BI)
                cols = slice(b * BI, (b + 1) * BI) if isinstance(b, int) else bass.ds(b * BI, BI)

                def then(ins, k):
                    ins.then_inc(dve_s, 1)
                    dve.wait_ge(dve_s, b * 3 + (c0 + k))

                nc.vector.tensor_scalar(posf[:, 1, :], rank[:], P // 2 - 0.5, None, ALU.is_gt)
                then(nc.vector.scalar_tensor_tensor(out=posf[:, 0, :], in0=rank[:], scalar=float(NT), in1=slot0[:, cols],
                                                    op0=ALU.mult, op1=ALU.add), 1)
                then(nc.vector.tensor_tensor(posf[:, 2, :], dump[:, cols], posf[:, 0, :], ALU.subtract), 2)
                then(nc.vector.tensor_tensor(posf[:, 2, :], posf[:, 2, :], posf[:, 1, :], ALU.mult), 3)
                nc.vector.tensor_tensor(posI[:, cols], posf[:, 0, :], posf[:, 2, :], ALU.add).then_inc(pos_ready, 1)

            edge_blocks(dve, slots)
            chain[0] = c0 + 3 * EB

            dve.wait_ge(cmp_done, NE)
            link(nc.vector.tensor_copy(tot[:], ps[:, 0, 0:NT]))
            link(nc.vector.tensor_tensor(tot[:], tot[:], ps[:, 1, 0:NT], ALU.max))
            link(nc.vector.tensor_reduce(tmax[:], tot[:], axis=AX, op=ALU.max))
            nc.vector.tensor_scalar(ovf[:], tmax[:], P // 2 + 0.5, None, ALU.is_gt).then_inc(ovf_ok, 1)
            link(nc.vector.tensor_scalar(rcnt[:], ps[:, 2, 0:NT], 1.0, None, ALU.max))
            nc.vector.reciprocal(rcnt[:], rcnt[:]).then_inc(rcnt_ok, 1)
            dve.wait_ge(rcnt_ok, 1)

            def merge(t, p):
                col = (lambda a: a[0:p, t:t + 1]) if isinstance(t, int) else (lambda a: a[:, bass.ds(t, 1)])

                def then(ins, k):
                    ins.then_inc(fch, 1)
                    dve.wait_ge(fch, t * 6 + k)

                wait(dve, f_done, 16 * t)
                key = f_key[0:p, 0:1]
                then(nc.vector.tensor_scalar(key, col(loF), float(NT), None, ALU.mult), 1)
                then(nc.vector.tensor_tensor(key, key, col(hiF), ALU.add), 2)
                nc.vector.tensor_copy(f_get[0:p, :], key)
                nc.vector.tensor_scalar(f_kb[0:p, :], lo1_row[0:p, :], 0.0, key, ALU.mult, ALU.add).then_inc(f_keys, 1)
                dve.wait_ge(f_row, t + 1)
                then(nc.vector.tensor_scalar(f_same[0:p, 0:p], ps[0:p, 6, 0:p], key, None, ALU.is_equal), 3)
                nc.vector.tensor_tensor(f_junk[0:p, 0:p], f_same[0:p, 0:p], f_earlier[0:p, 0:p], ALU.mult).then_inc(f_sameok, 1)
                dve.wait_ge(f_sameok, t + 1)
                then(nc.vector.tensor_reduce(f_key[0:p, 1:2], f_junk[0:p, 0:p], axis=AX, op=ALU.max), 4)
                then(nc.vector.tensor_scalar(f_key[0:p, 2:3], key, -1.0, dump[0:p, 0:1], ALU.mult, ALU.add), 5)
                then(nc.vector.tensor_tensor(f_key[0:p, 3:4], f_key[0:p, 1:2], f_key[0:p, 2:3], ALU.mult), 6)
                nc.vector.tensor_tensor(f_put[0:p, :], f_key[0:p, 3:4], key, ALU.add).then_inc(f_idx, 1)
                dve.wait_ge(f_got, 16 * (t + 1))
                dve.wait_ge(f_C, t + 1)
                nc.vector.tensor_scalar(f_new[0:p, D:RW], col(loF), 1.0, None, ALU.add)
                nc.vector.tensor_tensor(f_new[0:p, 0:D], ps[0:p, 7, 0:D], f_old[0:p, 0:D], ALU.add).then_inc(f_sum, 1)

            rebuild(dve, merge)

            def scale0(q, s):
                dve.wait_ge(mz_done, 2 * q + 2)
                pn = np_(q)
                r = (rcnt[0:pn, q * HT:(q + 1) * HT] if isinstance(q, int) else rcnt[:, bass.ds(q * HT, HT)])
                nc.vector.tensor_tensor(xr[0:pn, s, :].rearrange("n (i f) -> n i f", i=HT),
                                        ps[0:pn, 4 + s % 2, :].rearrange("n (i f) -> n i f", i=HT),
                                        r.unsqueeze(2).to_broadcast([pn, HT, D]), ALU.mult).then_inc(zs, 1)

            def add0(q, s):
                dve.wait_ge(zs, q + 1)
                dve.wait_ge(mx_done, q + 1)
                pn = np_(q)
                nc.vector.tensor_tensor(xr[0:pn, s, :], ps[0:pn, 2 + s % 2, :], xr[0:pn, s, :], ALU.add).then_inc(sum_ready, 1)

            def stat(l, q, ready):
                dve.wait_ge(ready, q + 1)
                dst = stats[:, q, :] if isinstance(q, int) else stats[:, bass.ds(q, 1), :].rearrange("p a c -> p (a c)")
                nc.vector.bn_stats(dst, hcol(q)).then_inc(stl[l], 1)

            def layer0(q, s):
                scale0(q, s)
                if not (isinstance(q, int) and q < 2):
                    stat(0, q - 2, h0_ready)
                add0(q, s)

            halves(dve, layer0)
            stat(0, NH - 2, h0_ready)
            stat(0, NH - 1, h0_ready)

            def batchnorm(l):
                dve.wait_ge(stl[l], NH)
                link(nc.vector.bn_aggr(agg[:], stats[:].rearrange("p a c -> p (a c)")))
                nc.vector.tensor_scalar(bn_t[:], agg[:, 1:2], EPS, None, ALU.add).then_inc(agg_ok, 1)
                dve.wait_ge(std_ok, l + 1)
                link(nc.vector.reciprocal(bn_std[:], bn_std[:]))
                link(nc.vector.tensor_tensor(bn_a[:, l:l + 1], bn_std[:], vecs[:, 4 + 2 * l:5 + 2 * l], ALU.mult))
                link(nc.vector.tensor_tensor(bn_t[:], agg[:, 0:1], bn_a[:, l:l + 1], ALU.mult))
                nc.vector.tensor_tensor(bn_c[:, l:l + 1], vecs[:, 5 + 2 * l:6 + 2 * l], bn_t[:], ALU.subtract).then_inc(ac_ok, 1)

            for l, W in ((1, W1T), (2, W2T)):
                batchnorm(l - 1)
                dve.wait_ge(bmm_ok, l)
                nc.vector.tensor_scalar(W[:], W[:], bn_a[:, l - 1:l], None, ALU.mult)
                nc.vector.tensor_tensor(bias[:, l:l + 1], ps[:, 7, 0:1], vecs[:, 1 + l:2 + l], ALU.add).then_inc(fold_ok, 1)
                halves(dve, lambda q, s: stat(l, q, hr[l]))
            batchnorm(2)

            def residual(q, s, it):
                dve.wait_ge(yT_done, q + 1)
                dve.wait_ge(x2_in[s], 16 * (q // PER + 1) if isinstance(q, int) else 16 * ((q - s) // PER + 1))
                pn = np_(q)
                nc.vector.tensor_tensor(xr[0:pn, s, :], ps[0:pn, 4 + s % 2, :], xr[0:pn, s, :], ALU.add).then_inc(res_ready, 1)

            def ln_stats(q, s):
                dve.wait_ge(res_ready, q + 1)
                pn = np_(q)
                for j in range(HT):
                    last = nc.vector.bn_stats(lnst[0:pn, s % 2, j, :], xr[0:pn, s, j * D:(j + 1) * D])
                last.then_inc(lnst_ok, 1)
                dve.wait_ge(lnst_ok, q + 1)
                wait(dve, ln_ready, q - 1)
                me, mo = lnst[0:pn, s % 2, :, 1], lnst[0:pn, s % 2, :, 4]
                ve, vo = lnst[0:pn, s % 2, :, 2], lnst[0:pn, s % 2, :, 5]
                o = 4 * (s % 2)
                mean, var, d, v = (lnm[0:pn, o + k, :] for k in (0, 1, 2, 3))

                def then(ins, k):
                    ins.then_inc(lch, 1)
                    dve.wait_ge(lch, q * 2 + k)

                nc.vector.tensor_tensor(mean, me, mo, ALU.add)
                nc.vector.tensor_tensor(v, ve, vo, ALU.add)
                then(nc.vector.tensor_tensor(d, me, mo, ALU.subtract), 1)
                nc.vector.tensor_scalar(mean, mean, 0.5, None, ALU.mult)
                nc.vector.tensor_scalar(v, v, 1.0 / D, EPS, ALU.mult, ALU.add)
                then(nc.vector.scalar_tensor_tensor(out=d, in0=d, scalar=0.25, in1=d, op0=ALU.mult, op1=ALU.mult), 2)
                nc.vector.tensor_tensor(var, v, d, ALU.add).then_inc(lnv_ok, 1)

            def ln_rstd(q, s):
                dve.wait_ge(lnsd_ok, q + 1)
                pn = np_(q)
                nc.vector.reciprocal(lnm[0:pn, 4 * (s % 2) + 3, :], lnm[0:pn, 4 * (s % 2) + 2, :]).then_inc(lnr_ok, 1)

            def final(q, s):
                residual(q, s, None)
                if not (isinstance(q, int) and q == 0):
                    ln_rstd(q - 1, (s - 1) % PER)
                ln_stats(q, s)

            halves(dve, final)
            ln_rstd(NH - 1, (NH - 1) % PER)

        @block.tensor
        def _(pe):
            pe.wait_ge(const_ok, 1)
            pe.wait_ge(w_in, 48)
            pe.wait_ge(v_in, 160)
            for k in range(4):
                nc.tensor.transpose(ps[:, 0, k * P:(k + 1) * P], wraw[:, k, :], ident[:])
            nc.tensor.transpose(ps[:, 1, 0:P], wraw[:, 4, :], ident[:])
            nc.tensor.transpose(ps[:, 1, P:P + 10], vraw[:, :], ident[0:10, 0:10]).then_inc(wT_done, 1)
            pe.wait_ge(wT_ready, 1)
            nc.tensor.matmul(ps[:, 2, 0:1], W0cT[:], vecs[:, 0:1], start=True, stop=True).then_inc(b0_done, 1)
            pe.wait_ge(bias_ok, 1)

            def transpose_edges(b, k):
                hf = 2 * b + k
                p = ep(b)
                wait(pe, eT_ready, hf - 1)
                for i in range(HT):
                    c = (k * HT + i) * D
                    last = nc.tensor.transpose(ps[:, 3 + k, i * P:i * P + p], er[0:p, transpose_edges.r, c:c + D], ident[0:p, 0:p])
                last.then_inc(eT_done, 1)

            def project(b, k):
                hf = 2 * b + k
                p = ep(b)
                pe.wait_ge(eT_ready, hf + 1)
                wait(pe, rows_ready, hf - 1)
                for i in range(HT):
                    last = nc.tensor.matmul(ps[0:p, 5 + k, i * D:(i + 1) * D], eT[:, k, i * P:i * P + p], W0bT[:],
                                            start=True, stop=True)
                last.then_inc(pj_done, 1)

            def count(b, r, n):
                p = ep(b)
                pe.wait_ge(e_in[r], 16 * n)
                transpose_edges.r = r
                last_tile = isinstance(b, int) and b == EBF
                for i in range(BI):
                    t = b * BI + i
                    first = isinstance(t, int) and t == 0
                    if i % HT == 0:
                        transpose_edges(b, i // HT)
                    pe.wait_ge(oh_ready, t + 1)
                    nc.tensor.matmul(ps[0:p, i % 2, 0:NT], before[0:p, 0:p], ohh[0:p, i % 4, :],
                                     start=isinstance(t, int) and t < 2, stop=False, skip_group_check=True).then_inc(tri_done, 1)
                    nc.tensor.matmul(ps[:, 2, 0:NT], ohl[0:p, i % 4, :], ohh[0:p, i % 4, :],
                                     start=first, stop=isinstance(t, int) and t == NE - 1, skip_group_check=True)
                    if not first:
                        rest(t - 1, (i - 1) % BI, ep(b) if i else P)
                    if i % HT == HT - 1:
                        project(b, i // HT)

            def rest(t, i, p):
                pe.wait_ge(rank_ready, t + 1)
                nc.tensor.matmul(ps[:, i % 2, 0:NT], notbefore[0:p, :], ohh[0:p, i % 4, :],
                                 start=False, stop=False, skip_group_check=True).then_inc(cmp_done, 1)

            for b in range(4):
                count(b, b, 1)
            with pe.Fori(1, EBF // 4) as it:
                for r in range(4):
                    count(it * 4 + r, r, it + 1)
            for b in range(EBF // 4 * 4, EB):
                count(b, b % 4, b // 4 + 1)
            rest(NE - 1, BI - 1, EPL)

            def xT(q, s):
                pe.wait_ge(x_in[s], 16 * (q // PER + 1) if isinstance(q, int) else 16 * ((q - s) // PER + 1))
                wait(pe, xT_ready, q - 1)
                pn = np_(q)
                for j in range(HT):
                    last = nc.tensor.transpose(ps[:, s % 2, j * P:j * P + pn], xr[0:pn, s, j * D:(j + 1) * D], ident[0:pn, 0:pn])
                last.then_inc(xT_done, 1)

            def mx(q, s):
                pe.wait_ge(xT_ready, q + 1)
                wait(pe, sum_ready, q - 1)
                pn = np_(q)
                for j in range(HT):
                    last = nc.tensor.matmul(ps[0:pn, 2 + s % 2, j * D:(j + 1) * D], stage[:, s % 2, j * P:j * P + pn], W0aT[:],
                                            start=True, stop=True)
                last.then_inc(mx_done, 1)

            def mz(q, s):
                pn = np_(q)
                for k in range(2):
                    pe.wait_ge(oh0_ready, 2 * q + k + 1)
                    for j in range(2):
                        t = 2 * k + j
                        c = ((s % 2) * HT + t) * RW
                        last = nc.tensor.matmul(ps[0:pn, 4 + s % 2, t * D:(t + 1) * D], oneh[:, k, j, 0:pn],
                                                tabr[:, s // 2, c:c + D], start=True, stop=True)
                    last.then_inc(mz_done, 1)

            def hT(q, s):
                pe.wait_ge(sum_ready, q + 1)
                wait(pe, h0_ready, q - 1)
                pn = np_(q)
                for j in range(HT):
                    last = nc.tensor.transpose(ps[:, 6 + s % 2, j * pn:(j + 1) * pn], xr[0:pn, s, j * D:(j + 1) * D],
                                               ident[0:pn, 0:pn])
                last.then_inc(hT_done, 1)

            pe.wait_ge(rcnt_ok, 1)

            def sums(t, p):
                pe.wait_ge(f_in, 16 * (t + 1))
                nc.tensor.transpose(ps[:, 3, 0:p], f_e[0:p, :], ident[0:p, 0:p]).then_inc(f_T, 1)
                pe.wait_ge(f_Tc, t + 1)
                nc.tensor.matmul(ps[0:p, 5, 0:D], f_eT[:, 0:p], W0bT[:], start=True, stop=True).then_inc(f_P, 1)
                pe.wait_ge(f_keys, t + 1)
                nc.tensor.matmul(ps[0:p, 6, 0:p], f_kb[0:p, 0:p], ident[0:p, 0:p], start=True, stop=True).then_inc(f_row, 1)
                pe.wait_ge(f_Pc, t + 1)
                pe.wait_ge(f_idx, t + 1)
                nc.tensor.matmul(ps[0:p, 7, 0:D], f_same[0:p, 0:p], f_p[0:p, :], start=True, stop=True).then_inc(f_C, 1)

            rebuild(pe, sums)
            xT(0, 0)

            def layer0(q, s):
                if not (isinstance(q, int) and q == NH - 1):
                    xT(q + 1, (s + 1) % PER)
                mx(q, s)
                mz(q, s)
                if not (isinstance(q, int) and q == 0):
                    hT(q - 1, (s - 1) % PER)

            halves(pe, layer0)
            hT(NH - 1, (NH - 1) % PER)

            for l, W in ((1, W1T), (2, W2T)):
                pe.wait_ge(ac_ok, l)
                nc.tensor.matmul(ps[:, 7, 0:1], W[:], bn_c[:, l - 1:l], start=True, stop=True).then_inc(bmm_ok, 1)
                pe.wait_ge(fold_ok, l)

                def layer(q, s):
                    wait(pe, hr[l], q - 3)
                    pn = np_(q)
                    nc.tensor.matmul(ps[:, s, 0:HT * pn], W[:], hcol(q), start=True, stop=True).then_inc(mm[l], 1)

                halves(pe, layer)

            def yT(q, s):
                pe.wait_ge(y_ready, q + 1)
                wait(pe, res_ready, q - 1)
                pn = np_(q)
                for j in range(HT):
                    last = nc.tensor.transpose(ps[0:pn, 4 + s % 2, j * P:(j + 1) * P], stage[:, s % 2, j * pn:(j + 1) * pn], ident[:])
                last.then_inc(yT_done, 1)

            halves(pe, yT)


_USED = ["x", "src", "edge_attr_128", "L0_gnn_u", "L0_gnn_W0", "L0_gnn_b0", "L0_gnn_W1", "L0_gnn_b1", "L0_gnn_W2", "L0_gnn_b2",
         "L0_gnn_g0", "L0_gnn_bt0", "L0_gnn_g1", "L0_gnn_bt1", "L0_gnn_g2", "L0_gnn_bt2"]


def kernel(**inputs):
    import numpy as _np
    import concourse.bacc as _bacc
    from concourse import mybir as _mybir
    from concourse.bass_utils import run_bass_kernel_spmd as _run

    nc = _bacc.Bacc("TRN2", target_bir_lowering=False, num_devices=1, dynamic_dma_scratch_size=2048)
    arrays, args = {}, []
    for name in _USED:
        a = _np.ascontiguousarray(inputs[name])
        arrays[f"in_{name}"] = a
        args.append(nc.dram_tensor(f"in_{name}", a.shape, _mybir.dt.from_np(a.dtype), kind="ExternalInput").ap())
    n = inputs["x"].shape[0]
    tiles = (n + 1023) // 1024 * 8
    table = nc.dram_tensor("edge_table", (128 * tiles + 128 * ((inputs["src"].shape[0] + 1023) // 1024 * 8), 129), _mybir.dt.float32, kind="Internal").ap()
    out = nc.dram_tensor("out", inputs["x"].shape, _mybir.dt.float32, kind="ExternalOutput").ap()
    gnn_resnorm_kernel(nc, *args, table, out)
    r = _run(nc, [arrays], core_ids=[0])
    return r.results[0]["out"]
```

```python
import concourse.bass as bass
from concourse import mybir
from contextlib import ExitStack


def gnn_resnorm_kernel(nc, x, src, edge_attr, u, W0, b0, W1, b1, W2, b2, g0, bt0, g1, bt1, g2, bt2, table, out):
    fp32, bf16, fp16, i32 = mybir.dt.float32, mybir.dt.bfloat16, mybir.dt.float16, mybir.dt.int32
    ALU = mybir.AluOpType
    ACT = mybir.ActivationFunctionType
    AX = mybir.AxisListType.X

    N, D = x.shape
    E = edge_attr.shape[0]
    P = 128
    BI = 8
    BN = P * BI
    NBF = N // BN
    PL = (N - NBF * BN) // BI
    NB = NBF + 1
    NT = NB * BI
    HT = 4
    HC = HT * P
    NH = 2 * NB
    NHF = 2 * NBF
    EBF = E // BN
    ET = EBF * BI
    EPL = (E - EBF * BN) // BI
    EB = EBF + 1
    NE = EB * BI
    RW = D + 1
    SLOTS = P * NT
    ZT = 14
    NZ = NT // ZT
    EPS = 1e-5
    PER = 4
    assert N % BI == 0 and E % BI == 0 and NT % ZT == 0 and NHF % PER == 0 and 0 < PL < P and 0 < EPL < P

    x_full = x[0:NBF * BN, :].rearrange("(g p s i) f -> p s g (i f)", p=P, s=2, i=HT)
    x_last = x[NBF * BN:N, :].rearrange("(p s i) f -> p s (i f)", s=2, i=HT)
    o_full = out[0:NBF * BN, :].rearrange("(g p s i) f -> p s g (i f)", p=P, s=2, i=HT)
    o_last = out[NBF * BN:N, :].rearrange("(p s i) f -> p s (i f)", s=2, i=HT)
    e_full = edge_attr[0:EBF * BN, :].rearrange("(p t) f -> p (t f)", p=P)
    e_last = edge_attr[EBF * BN:E, :].rearrange("(p t) f -> p (t f)", t=BI)
    src_full = src[0:EBF * BN].rearrange("(p t) -> p t", p=P)
    src_last = src[EBF * BN:E].rearrange("(p t) -> p t", t=BI)
    tab = table[0:SLOTS, :].rearrange("(p j) c -> p (j c)", p=P)

    ctx = ExitStack()
    with ctx:
        def sb(name, shape, dt=fp32, where=ctx):
            return where.enter_context(nc.sbuf_tensor(name, shape, dt))

        def sem(name):
            return ctx.enter_context(nc.semaphore(name))

        ident = sb("ident", [P, P])
        lo1_row = sb("lo1_row", [P, P])
        W0aT = sb("W0aT", [P, P])
        W1T = sb("W1T", [P, P])
        W2T = sb("W2T", [P, P])
        vecs = sb("vecs", [P, 10])
        rcnt = sb("rcnt", [P, NT])
        stats = sb("stats", [P, NH, 6])
        agg = sb("agg", [P, 2])
        bn_std = sb("bn_std", [P, 1])
        bn_a = sb("bn_a", [P, 3])
        bn_c = sb("bn_c", [P, 3])
        bn_t = sb("bn_t", [P, 1])
        bias = sb("bias", [P, 3])
        ovf = sb("ovf", [P, 1], i32)
        xr = sb("xr", [P, 4, HC])
        tabr = sb("tabr", [P, 2, BI * RW])
        stage = sb("stage", [P, 2, HC])
        oneh = sb("oneh", [P, 2, 2, P])
        lnst = sb("lnst", [P, 2, HT, 6])
        lnm = sb("lnm", [P, PER, 5, HT])
        h_last = tabr[:, 1, 0:BI * PL]

        ps = ctx.enter_context(nc.psum_tensor("ps", [P, 8, 512], fp32))

        sa = ExitStack()
        with sa:
            rows = sb("rows", [P, NE, RW], where=sa)
            er = sb("er", [P, 4, BI * D], where=sa)
            eT = sb("eT", [P, 2, 512], where=sa)
            hi_row = sb("hi_row", [P, NT], fp16, sa)
            iot = sb("iot", [P, NT], i32, sa)
            pidx_i = sb("pidx_i", [P, 1], i32, sa)
            pidx = sb("pidx", [P, 1], fp32, sa)
            lo_row = sb("lo_row", [P, P], fp16, sa)
            ohh = sb("ohh", [P, 4, NT], bf16, sa)
            ohl = sb("ohl", [P, 4, P], bf16, sa)
            junk = sb("junk", [P, 2, NT], bf16, sa)
            before = sb("before", [P, P], bf16, sa)
            notbefore = sb("notbefore", [P, P], bf16, sa)
            srcI = sb("srcI", [P, NE], i32, sa)
            t1 = sb("t1", [P, NE], i32, sa)
            t2 = sb("t2", [P, NE], i32, sa)
            t3 = sb("t3", [P, NE], i32, sa)
            hiF = sb("hiF", [P, NE], fp32, sa)
            loF = sb("loF", [P, NE], fp32, sa)
            rank = sb("rank", [P, BI], fp32, sa)
            slot0 = sb("slot0", [P, NE], fp32, sa)
            dump_i = sb("dump_i", [P, NE], i32, sa)
            dump = sb("dump", [P, NE], fp32, sa)
            posf = sb("posf", [P, 4, BI], fp32, sa)
            posI = sb("posI", [P, NE], i32, sa)
            zero = sb("zero", [P, ZT * RW], fp32, sa)
            wraw = sb("wraw", [P, 5, P], fp32, sa)
            vraw = sb("vraw", [10, P], fp32, sa)
            W0bT = sb("W0bT", [P, P], fp32, sa)
            W0cT = sb("W0cT", [P, P], fp32, sa)
            tot = sb("tot", [P, NT], fp32, sa)
            tmax = sb("tmax", [P, 1], fp32, sa)
            f_e = sb("f_e", [P, D], fp32, sa)
            f_eT = sb("f_eT", [P, P], fp32, sa)
            f_p = sb("f_p", [P, D], fp32, sa)
            f_key = sb("f_key", [P, 4], fp32, sa)
            f_get = sb("f_get", [P, 1], i32, sa)
            f_put = sb("f_put", [P, 1], i32, sa)
            f_kb = sb("f_kb", [P, P], fp32, sa)
            f_same = sb("f_same", [P, P], fp32, sa)
            f_earlier = sb("f_earlier", [P, P], fp32, sa)
            f_junk = sb("f_junk", [P, P], fp32, sa)
            f_old = sb("f_old", [P, RW], fp32, sa)
            f_new = sb("f_new", [P, RW], fp32, sa)
        h = sb("h", [P, NHF * HC])

        w_in, v_in, src_in, zero_done, scat_done = (
            sem("w_in"), sem("v_in"), sem("src_in"), sem("zero_done"), sem("scat_done"))
        e_in = [sem(f"e_in{i}") for i in range(4)]
        x_in = [sem(f"x_in{i}") for i in range(4)]
        x2_in = [sem(f"x2_in{i}") for i in range(4)]
        tab_in = [sem(f"tab_in{i}") for i in range(2)]
        out_w = [sem(f"out_w{i}") for i in range(4)]
        iota_ok, zero_ok, const_ok, srcset, meta_ok = (
            sem("iota_ok"), sem("zero_ok"), sem("const_ok"), sem("srcset"), sem("meta_ok"))
        wT_done, wT_ready, b0_done, bias_ok = sem("wT_done"), sem("wT_ready"), sem("b0_done"), sem("bias_ok")
        oh_ready, tri_done, rank_ready, cmp_done, pos_ready = (
            sem("oh_ready"), sem("tri_done"), sem("rank_ready"), sem("cmp_done"), sem("pos_ready"))
        eT_done, eT_ready, pj_done, rows_ready = sem("eT_done"), sem("eT_ready"), sem("pj_done"), sem("rows_ready")
        dve_s, ovf_ok, rcnt_ok = sem("dve_s"), sem("ovf_ok"), sem("rcnt_ok")
        turn = sem("turn")
        xT_done, xT_ready, mx_done, oh0_ready, mz_done, mx_ready, sum_ready, hT_done, h0_ready, st0 = (
            sem("xT_done"), sem("xT_ready"), sem("mx_done"), sem("oh0_ready"), sem("mz_done"), sem("mx_ready"),
            sem("sum_ready"), sem("hT_done"), sem("h0_ready"), sem("st0"))
        f_zero, f_in, f_got, f_done = sem("f_zero"), sem("f_in"), sem("f_got"), sem("f_done")
        f_T, f_Tc, f_P, f_Pc, f_keys, f_row, f_idx, f_C, f_sum, fch = (
            sem("f_T"), sem("f_Tc"), sem("f_P"), sem("f_Pc"), sem("f_keys"), sem("f_row"), sem("f_idx"), sem("f_C"),
            sem("f_sum"), sem("fch"))
        f_sameok = sem("f_sameok")
        lnrs_ok = sem("lnrs_ok")
        mm = [None, sem("mm1"), sem("mm2")]
        hr = [None, sem("hr1"), sem("hr2")]
        stl = [st0, sem("st1"), sem("st2")]
        agg_ok, std_ok, fold_ok, bmm_ok, ac_ok, bch = (
            sem("agg_ok"), sem("std_ok"), sem("fold_ok"), sem("bmm_ok"), sem("ac_ok"), sem("bch"))
        y_ready, yT_done, res_ready, lnst_ok, lnv_ok, lnsd_ok, lnr_ok, ln_ready, lch = (
            sem("y_ready"), sem("yT_done"), sem("res_ready"), sem("lnst_ok"), sem("lnv_ok"), sem("lnsd_ok"),
            sem("lnr_ok"), sem("ln_ready"), sem("lch"))

        def wait(eng, s, n):
            if not (isinstance(n, int) and n <= 0):
                eng.wait_ge(s, n)

        def np_(q):
            return PL if isinstance(q, int) and q >= NHF else P

        def hcol(q):
            if isinstance(q, int) and q >= NHF:
                return h_last[:, (q - NHF) * HT * PL:(q - NHF + 1) * HT * PL]
            return h[:, bass.ds(q * HC, HC)] if not isinstance(q, int) else h[:, q * HC:(q + 1) * HC]

        def zcol(q):
            if isinstance(q, int):
                return xr[:, q, :] if q < PER else h[:, (q - PER) * HC:(q - PER + 1) * HC]
            return h[:, bass.ds((q - PER) * HC, HC)]

        def halves(eng, step, peel=1):
            for q in range(peel * PER):
                step(q, q % PER)
            with eng.Fori(peel, NHF // PER - 1) as it:
                for s in range(PER):
                    step(it * PER + s, s)
            for q in range(NHF - PER, NH):
                step(q, q % PER)

        def edge_blocks(eng, step):
            step(0)
            with eng.Fori(1, EBF) as b:
                step(b)
            step(EBF)

        def ep(b):
            return EPL if isinstance(b, int) and b == EBF else P

        def rebuild(eng, step):
            eng.wait_ge(ovf_ok, 1)
            full = eng.value_load(ovf[0:1, 0:1], min_val=0, max_val=1)
            with eng.If(full):
                with eng.Fori(0, ET) as t:
                    step(t, P)
                for t in range(ET, NE):
                    step(t, EPL)
                eng.wait_ge(f_done, 16 * NE)

        block = ctx.enter_context(nc.Block())

        @block.sync
        def _(sp):
            sp.wait_ge(srcset, 1)
            sp.dma_start(srcI[:, 0:ET], src_full).then_inc(src_in, 16)
            sp.dma_start(srcI[0:EPL, ET:NE], src_last).then_inc(src_in, 16)
            sp.dma_start(wraw[:, 0:3, :].rearrange("p a b -> p (a b)"), W0).then_inc(w_in, 16)
            sp.dma_start(wraw[:, 3, :], W1).then_inc(w_in, 16)
            sp.dma_start(wraw[:, 4, :], W2).then_inc(w_in, 16)
            for k, v in enumerate((None, b0, b1, b2, g0, bt0, g1, bt1, g2, bt2)):
                sp.dma_start(vraw[k:k + 1, :], u[0:1, :] if k == 0 else v.rearrange("(a b) -> a b", a=1)).then_inc(v_in, 16)

            def load_edges(b, r):
                wait(sp, eT_done, 2 * (b - 3))
                if isinstance(b, int) and b == EBF:
                    sp.dma_start(er[0:EPL, r, :], e_last).then_inc(e_in[r], 16)
                else:
                    cols = (slice(b * BN, (b + 1) * BN) if isinstance(b, int) else bass.ds(b * BN, BN))
                    sp.dma_start(er[:, r, :], e_full[:, cols]).then_inc(e_in[r], 16)

            for b in range(4):
                load_edges(b, b)
            with sp.Fori(1, EBF // 4) as it:
                for r in range(4):
                    load_edges(it * 4 + r, r)
            for b in range(EBF // 4 * 4, EB):
                load_edges(b, b % 4)

            def load_x(q, s):
                wait(sp, hT_done, q - 3)
                if isinstance(q, int) and q >= NHF:
                    sp.dma_start(xr[0:PL, s, :], x_last[:, q % 2, :]).then_inc(x_in[s], 16)
                else:
                    g = q // 2 if isinstance(q, int) else None
                    sp.dma_start(xr[:, s, :], x_full[:, s % 2, g, :]).then_inc(x_in[s], 16)

            def load_x_dyn(it, s):
                q = it * PER + s
                wait(sp, hT_done, q - 3)
                sp.dma_start(xr[:, s, :], x_full[:, s % 2, bass.ds(it * 2 + s // 2, 1), :]).then_inc(x_in[s], 16)

            def load_table(g, r):
                wait(sp, mz_done, 4 * (g - 1))
                cols = (slice(g * BI * RW, (g + 1) * BI * RW) if isinstance(g, int) else bass.ds(g * (BI * RW), BI * RW))
                sp.dma_start(tabr[:, r, :], tab[:, cols]).then_inc(tab_in[r], 16)

            for q in range(PER):
                load_x(q, q)
            sp.wait_ge(scat_done, 16 * NE)

            def fetch(t, p):
                wait(sp, f_done, 16 * t)
                v = e_last[:, (t - ET) * D:(t - ET + 1) * D] if isinstance(t, int) else e_full[:, bass.ds(t * D, D)]
                sp.dma_start(f_e[0:p, :], v).then_inc(f_in, 16)

            rebuild(sp, fetch)
            load_table(0, 0)
            load_table(1, 1)
            with sp.Fori(1, NHF // PER) as it:
                for s in range(PER):
                    load_x_dyn(it, s)
                    if s % 2:
                        load_table(it * 2 + s // 2, s // 2)
            for q in range(NHF, NH):
                load_x(q, q % PER)
            load_table(NBF, 0)

            def load_x2(q, s, g):
                wait(sp, res_ready, q - 3)
                if isinstance(q, int):
                    v = x_last[:, q % 2, :] if q >= NHF else x_full[:, s % 2, g, :]
                    sp.dma_start(zcol(q)[0:np_(q), :], v).then_inc(x2_in[s], 16)
                else:
                    sp.dma_start(zcol(q), x_full[:, s % 2, bass.ds(g, 1), :]).then_inc(x2_in[s], 16)

            def store(q, s, g):
                sp.wait_ge(ln_ready, q + 1)
                if isinstance(q, int):
                    v = o_last[:, q % 2, :] if q >= NHF else o_full[:, s % 2, g, :]
                    sp.dma_start(v, zcol(q)[0:np_(q), :]).then_inc(out_w[s], 16)
                else:
                    sp.dma_start(o_full[:, s % 2, bass.ds(g, 1), :], zcol(q)).then_inc(out_w[s], 16)

            sp.wait_ge(hT_done, NH)
            for q in range(2 * PER):
                load_x2(q, q % PER, q // 2)
                if q >= PER:
                    store(q - PER, q - PER, (q - PER) // 2)
            with sp.Fori(1, NHF // PER - 1) as it:
                for s in range(PER):
                    load_x2(it * PER + (s + PER), s, it * 2 + (s // 2 + 2))
                    store(it * PER + s, s, it * 2 + s // 2)
            for q in range(NHF - PER, NH):
                if q + PER < NH:
                    load_x2(q + PER, q % PER, q // 2 + 2)
                store(q, q % PER, q // 2)
            for s in range(PER):
                sp.wait_ge(out_w[s], 16 * len(range(s, NH, PER)))

        @block.gpsimd
        def _(pool):
            nc.gpsimd.memset(srcI[:, ET:NE], 0).then_inc(srcset, 1)
            nc.gpsimd.memset(zero[:], 0.0).then_inc(zero_ok, 1)
            nc.gpsimd.iota(iot[:], [[1, NT]], base=0, channel_multiplier=0).then_inc(iota_ok, 1)
            nc.gpsimd.iota(pidx_i[:], [[0, 1]], base=0, channel_multiplier=1).then_inc(iota_ok, 1)
            nc.gpsimd.iota(dump_i[:], [[P, NE]], base=SLOTS, channel_multiplier=1).then_inc(iota_ok, 1)
            pool.wait_ge(zero_ok, 1)
            for z in range(NZ):
                pool.dma_start(tab[:, z * ZT * RW:(z + 1) * ZT * RW], zero[:]).then_inc(zero_done, 16)
            pool.wait_ge(zero_done, 16 * NZ)

            for b in range(EB):
                pool.wait_ge(pos_ready, b + 1)
                pool.wait_ge(rows_ready, 2 * (b + 1))
                p = ep(b)
                for t in range(b * BI, (b + 1) * BI):
                    pool.indirect_dma_start(
                        out=table[:, :], out_offset=bass.IndirectOffsetOnAxis(ap=posI[0:p, t:t + 1], axis=0),
                        in_=rows[0:p, t, :], in_offset=None).then_inc(scat_done, 16)

            def gather_scatter(t, p):
                pool.wait_ge(f_zero, 16 * NZ)
                wait(pool, f_done, 16 * t)
                pool.wait_ge(f_idx, t + 1)
                pool.sem_inc(turn, 1)
                pool.indirect_dma_start(out=f_old[0:p, :], out_offset=None, in_=table[0:SLOTS, :],
                                        in_offset=bass.IndirectOffsetOnAxis(ap=f_get[0:p, 0:1], axis=0)).then_inc(f_got, 16)
                pool.wait_ge(f_sum, t + 1)
                pool.sem_inc(turn, 1)
                pool.indirect_dma_start(out=table[:, :], out_offset=bass.IndirectOffsetOnAxis(ap=f_put[0:p, 0:1], axis=0),
                                        in_=f_new[0:p, :], in_offset=None).then_inc(f_done, 16)

            pool.wait_ge(ovf_ok, 1)
            with pool.If(pool.value_load(ovf[0:1, 0:1], min_val=0, max_val=1)):
                pool.wait_ge(scat_done, 16 * NE)
                for z in range(NZ):
                    pool.dma_start(tab[:, z * ZT * RW:(z + 1) * ZT * RW], zero[:]).then_inc(f_zero, 16)
            rebuild(pool, gather_scatter)


        @block.scalar
        def _(act):
            def project(b):
                for k in range(2):
                    hf = 2 * b + k
                    p = ep(b)
                    act.wait_ge(eT_done, hf + 1)
                    wait(act, pj_done, hf - 1)
                    nc.scalar.activation(eT[:, k, :].rearrange("f (i e) -> f i e", i=HT)[:, :, 0:p],
                                         ps[:, 3 + k, :].rearrange("f (i e) -> f i e", i=HT)[:, :, 0:p],
                                         ACT.Copy).then_inc(eT_ready, 1)
                    act.wait_ge(pj_done, hf + 1)
                    t = hf * HT
                    dst = rows[0:p, t:t + HT, 0:D] if isinstance(t, int) else rows[:, bass.ds(t, HT), 0:D]
                    nc.scalar.activation(dst, ps[0:p, 5 + k, :].rearrange("e (i f) -> e i f", i=HT),
                                         ACT.Copy).then_inc(rows_ready, 1)

            edge_blocks(act, project)

            def copies(t, p):
                act.wait_ge(f_T, t + 1)
                nc.scalar.activation(f_eT[:, 0:p], ps[:, 3, 0:p], ACT.Copy).then_inc(f_Tc, 1)
                act.wait_ge(f_P, t + 1)
                nc.scalar.activation(f_p[0:p, :], ps[0:p, 5, 0:D], ACT.Copy).then_inc(f_Pc, 1)

            rebuild(act, copies)

            def copy_xT(q, s):
                act.wait_ge(xT_done, q + 1)
                wait(act, mx_done, q - 1)
                pn = np_(q)
                nc.scalar.activation(stage[:, s % 2, :].rearrange("f (i e) -> f i e", i=HT)[:, :, 0:pn],
                                     ps[:, s % 2, :].rearrange("f (i e) -> f i e", i=HT)[:, :, 0:pn],
                                     ACT.Copy).then_inc(xT_ready, 1)

            def copy_mx(q, s):
                act.wait_ge(mx_done, q + 1)
                pn = np_(q)
                nc.scalar.activation(xr[0:pn, s, :], ps[0:pn, 2 + s % 2, :], ACT.Copy).then_inc(mx_ready, 1)

            def relu0(q, s):
                act.wait_ge(hT_done, q + 1)
                pn = np_(q)
                nc.scalar.activation(hcol(q), ps[:, 6 + s % 2, 0:HT * pn], ACT.Relu, bias=bias[:, 0:1]).then_inc(h0_ready, 1)

            act.wait_ge(bias_ok, 1)
            copy_xT(0, 0)

            def layer0(q, s):
                if not (isinstance(q, int) and q == NH - 1):
                    copy_xT(q + 1, (s + 1) % PER)
                copy_mx(q, s)
                if not (isinstance(q, int) and q == 0):
                    relu0(q - 1, (s - 1) % PER)

            halves(act, layer0)
            relu0(NH - 1, (NH - 1) % PER)

            def bn_sqrt(l):
                act.wait_ge(agg_ok, l + 1)
                nc.scalar.activation(bn_std[:], bn_t[:], ACT.Sqrt).then_inc(std_ok, 1)

            bn_sqrt(0)
            for l in (1, 2):
                act.wait_ge(fold_ok, l)

                def layer(q, s):
                    act.wait_ge(mm[l], q + 1)
                    pn = np_(q)
                    nc.scalar.activation(hcol(q), ps[:, s, 0:HT * pn], ACT.Relu, bias=bias[:, l:l + 1]).then_inc(hr[l], 1)

                halves(act, layer)
                bn_sqrt(l)

            act.wait_ge(ac_ok, 3)

            def normalise(q, s):
                wait(act, yT_done, q - 1)
                pn = np_(q)
                nc.scalar.activation(stage[:, s % 2, 0:HT * pn], hcol(q), ACT.Identity,
                                     bias=bn_c[:, 2:3], scale=bn_a[:, 2:3]).then_inc(y_ready, 1)

            def ln_sqrt(q, s):
                act.wait_ge(lnv_ok, q + 1)
                pn = np_(q)
                nc.scalar.activation(lnm[0:pn, s, 2, :], lnm[0:pn, s, 1, :], ACT.Sqrt).then_inc(lnsd_ok, 1)

            def ln_apply(q, s):
                act.wait_ge(lnr_ok, q + 1)
                pn = np_(q)
                z = zcol(q)
                for j in range(HT):
                    v = z[0:pn, j * D:(j + 1) * D]
                    last = nc.scalar.activation(v, v, ACT.Identity, bias=lnm[0:pn, s, 4, j:j + 1], scale=lnm[0:pn, s, 3, j:j + 1])
                last.then_inc(ln_ready, 1)

            normalise(0, 0)

            def final(q, s):
                if not (isinstance(q, int) and q == NH - 1):
                    normalise(q + 1, (s + 1) % PER)
                if not (isinstance(q, int) and q < 2):
                    ln_apply(q - 2, (s - 2) % PER)
                if not (isinstance(q, int) and q == 0):
                    ln_sqrt(q - 1, (s - 1) % PER)

            halves(act, final, peel=2)
            ln_apply(NH - 2, (NH - 2) % PER)
            ln_sqrt(NH - 1, (NH - 1) % PER)
            ln_apply(NH - 1, (NH - 1) % PER)

        @block.vector
        def _(dve):
            chain = [0]

            def link(ins):
                chain[0] += 1
                ins.then_inc(dve_s, 1)
                dve.wait_ge(dve_s, chain[0])

            dve.wait_ge(iota_ok, 3)
            nc.vector.tensor_copy(hi_row[:], iot[:])
            nc.vector.tensor_copy(lo_row[:], iot[:, 0:P])
            nc.vector.tensor_scalar(lo1_row[:], iot[:, 0:P], 1.0, None, ALU.add)
            link(nc.vector.tensor_copy(pidx[:], pidx_i[:]))
            nc.vector.tensor_scalar(ident[:], lo_row[:], pidx[:, 0:1], None, ALU.is_equal)
            nc.vector.tensor_scalar(before[:], lo_row[:], pidx[:, 0:1], None, ALU.is_gt)
            nc.vector.tensor_scalar(notbefore[:], lo_row[:], pidx[:, 0:1], None, ALU.is_le)
            nc.vector.tensor_scalar(f_earlier[:], lo_row[:], pidx[:, 0:1], None, ALU.is_lt)
            nc.vector.tensor_copy(dump[:], dump_i[:]).then_inc(const_ok, 1)

            dve.wait_ge(src_in, 32)
            nc.vector.tensor_scalar(t1[:], srcI[:], 7, 0x1FFFFF8, ALU.logical_shift_right, ALU.bitwise_and)
            nc.vector.tensor_scalar(t2[:], srcI[:], 7, None, ALU.bitwise_and)
            link(nc.vector.tensor_scalar(t3[:], srcI[:], 3, 127, ALU.logical_shift_right, ALU.bitwise_and))
            nc.vector.tensor_copy(loF[:], t3[:])
            link(nc.vector.tensor_tensor(hiF[:], t1[:], t2[:], ALU.add))
            nc.vector.tensor_scalar(slot0[:].rearrange("p (a b) -> p a b", b=2)[:, :, 1],
                                    hiF[:].rearrange("p (a b) -> p a b", b=2)[:, :, 1], float(P // 2 * NT), None, ALU.add)
            nc.vector.tensor_copy(slot0[:].rearrange("p (a b) -> p a b", b=2)[:, :, 0],
                                  hiF[:].rearrange("p (a b) -> p a b", b=2)[:, :, 0])
            nc.vector.tensor_scalar(rows[:, :, D:D + 1].rearrange("p t a -> p (t a)"), loF[:], 1.0, None,
                                    ALU.add).then_inc(meta_ok, 1)
            dve.wait_ge(meta_ok, 1)

            dve.wait_ge(wT_done, 1)
            for dst, bank, k in ((W0aT, 0, 0), (W0bT, 0, 1), (W0cT, 0, 2), (W1T, 0, 3), (W2T, 1, 0)):
                nc.vector.tensor_copy(dst[:], ps[:, bank, k * P:(k + 1) * P])
            nc.vector.tensor_copy(vecs[:], ps[:, 1, P:P + 10]).then_inc(wT_ready, 1)
            dve.wait_ge(b0_done, 1)
            dve.wait_ge(wT_ready, 1)
            nc.vector.tensor_tensor(bias[:, 0:1], ps[:, 2, 0:1], vecs[:, 1:2], ALU.add).then_inc(bias_ok, 1)

            def onehot(t, i, p):
                wait(dve, cmp_done, t - 3)
                r = i % 4
                sc = (lambda a: a[0:p, t:t + 1]) if isinstance(t, int) else (lambda a: a[:, bass.ds(t, 1)])
                nc.vector.tensor_scalar(ohh[0:p, r, :], hi_row[0:p, :], sc(hiF), None, ALU.is_equal)
                nc.vector.tensor_scalar(ohl[0:p, r, :], lo_row[0:p, :], sc(loF), None, ALU.is_equal).then_inc(oh_ready, 1)

            def select(t, i, p):
                dve.wait_ge(tri_done, t + 1)
                nc.vector.tensor_tensor_reduce(out=junk[0:p, i % 2, :], in0=ohh[0:p, i % 4, :], in1=ps[0:p, i % 2, 0:NT],
                                               scale=1.0, scalar=0.0, op0=ALU.mult, op1=ALU.add,
                                               accum_out=rank[0:p, i:i + 1]).then_inc(rank_ready, 1)

            link(nc.vector.memset(rank[:], 0.0))
            onehot(0, 0, P)
            c0 = chain[0]

            def slots(b):
                p, pn = ep(b), ep(b + 1 if isinstance(b, int) else b)
                for i in range(BI):
                    t = b * BI + i
                    if not (isinstance(t, int) and t == NE - 1):
                        onehot(t + 1, (i + 1) % BI, pn if i == BI - 1 else p)
                    select(t, i, p)
                dve.wait_ge(rank_ready, (b + 1) * BI)
                cols = slice(b * BI, (b + 1) * BI) if isinstance(b, int) else bass.ds(b * BI, BI)

                def then(ins, k):
                    ins.then_inc(dve_s, 1)
                    dve.wait_ge(dve_s, b * 3 + (c0 + k))

                nc.vector.tensor_scalar(posf[:, 1, :], rank[:], P // 2 - 0.5, None, ALU.is_gt)
                then(nc.vector.scalar_tensor_tensor(out=posf[:, 0, :], in0=rank[:], scalar=float(NT), in1=slot0[:, cols],
                                                    op0=ALU.mult, op1=ALU.add), 1)
                then(nc.vector.tensor_tensor(posf[:, 2, :], dump[:, cols], posf[:, 0, :], ALU.subtract), 2)
                then(nc.vector.tensor_tensor(posf[:, 2, :], posf[:, 2, :], posf[:, 1, :], ALU.mult), 3)
                nc.vector.tensor_tensor(posI[:, cols], posf[:, 0, :], posf[:, 2, :], ALU.add).then_inc(pos_ready, 1)

            edge_blocks(dve, slots)
            chain[0] = c0 + 3 * EB

            dve.wait_ge(cmp_done, NE)
            link(nc.vector.tensor_copy(tot[:], ps[:, 0, 0:NT]))
            link(nc.vector.tensor_tensor(tot[:], tot[:], ps[:, 1, 0:NT], ALU.max))
            link(nc.vector.tensor_reduce(tmax[:], tot[:], axis=AX, op=ALU.max))
            nc.vector.tensor_scalar(ovf[:], tmax[:], P // 2 + 0.5, None, ALU.is_gt).then_inc(ovf_ok, 1)
            link(nc.vector.tensor_scalar(rcnt[:], ps[:, 2, 0:NT], 1.0, None, ALU.max))
            nc.vector.reciprocal(rcnt[:], rcnt[:]).then_inc(rcnt_ok, 1)
            dve.wait_ge(rcnt_ok, 1)

            def merge(t, p):
                col = (lambda a: a[0:p, t:t + 1]) if isinstance(t, int) else (lambda a: a[:, bass.ds(t, 1)])

                def then(ins, k):
                    ins.then_inc(fch, 1)
                    dve.wait_ge(fch, t * 6 + k)

                wait(dve, f_done, 16 * t)
                key = f_key[0:p, 0:1]
                then(nc.vector.tensor_scalar(key, col(loF), float(NT), None, ALU.mult), 1)
                then(nc.vector.tensor_tensor(key, key, col(hiF), ALU.add), 2)
                nc.vector.tensor_copy(f_get[0:p, :], key)
                nc.vector.tensor_scalar(f_kb[0:p, :], lo1_row[0:p, :], 0.0, key, ALU.mult, ALU.add).then_inc(f_keys, 1)
                dve.wait_ge(f_row, t + 1)
                then(nc.vector.tensor_scalar(f_same[0:p, 0:p], ps[0:p, 6, 0:p], key, None, ALU.is_equal), 3)
                nc.vector.tensor_tensor(f_junk[0:p, 0:p], f_same[0:p, 0:p], f_earlier[0:p, 0:p], ALU.mult).then_inc(f_sameok, 1)
                dve.wait_ge(f_sameok, t + 1)
                then(nc.vector.tensor_reduce(f_key[0:p, 1:2], f_junk[0:p, 0:p], axis=AX, op=ALU.max), 4)
                then(nc.vector.tensor_scalar(f_key[0:p, 2:3], key, -1.0, dump[0:p, 0:1], ALU.mult, ALU.add), 5)
                then(nc.vector.tensor_tensor(f_key[0:p, 3:4], f_key[0:p, 1:2], f_key[0:p, 2:3], ALU.mult), 6)
                nc.vector.tensor_tensor(f_put[0:p, :], f_key[0:p, 3:4], key, ALU.add).then_inc(f_idx, 1)
                dve.wait_ge(f_got, 16 * (t + 1))
                dve.wait_ge(f_C, t + 1)
                nc.vector.tensor_scalar(f_new[0:p, D:RW], col(loF), 1.0, None, ALU.add)
                nc.vector.tensor_tensor(f_new[0:p, 0:D], ps[0:p, 7, 0:D], f_old[0:p, 0:D], ALU.add).then_inc(f_sum, 1)

            rebuild(dve, merge)

            def onehots(q, s):
                g2 = s // 2
                dve.wait_ge(tab_in[g2], 16 * (q // PER + 1) if isinstance(q, int) else 16 * ((q - s) // PER + 1))
                pn = np_(q)
                for k in range(2):
                    wait(dve, mz_done, 2 * q + k - 1)
                    for j in range(2):
                        i = (s % 2) * HT + 2 * k + j
                        last = nc.vector.tensor_scalar(oneh[:, k, j, 0:pn], lo1_row[:, 0:pn],
                                                       tabr[:, g2, i * RW + D:i * RW + D + 1], None, ALU.is_equal)
                    last.then_inc(oh0_ready, 1)

            def combine0(q, s):
                dve.wait_ge(mz_done, 2 * q + 2)
                dve.wait_ge(mx_ready, q + 1)
                pn = np_(q)
                for j in range(HT):
                    t = q * HT + j
                    v = xr[0:pn, s, j * D:(j + 1) * D]
                    last = nc.vector.scalar_tensor_tensor(
                        out=v, in0=ps[0:pn, 4 + s % 2, j * D:(j + 1) * D],
                        scalar=rcnt[0:pn, t:t + 1] if isinstance(q, int) else rcnt[:, bass.ds(t, 1)],
                        in1=v, op0=ALU.mult, op1=ALU.add)
                last.then_inc(sum_ready, 1)

            def stat(l, q, ready):
                dve.wait_ge(ready, q + 1)
                dst = stats[:, q, :] if isinstance(q, int) else stats[:, bass.ds(q, 1), :].rearrange("p a c -> p (a c)")
                nc.vector.bn_stats(dst, hcol(q)).then_inc(stl[l], 1)

            onehots(0, 0)

            def layer0(q, s):
                if not (isinstance(q, int) and q == NH - 1):
                    onehots(q + 1, (s + 1) % PER)
                combine0(q, s)
                if not (isinstance(q, int) and q < 2):
                    stat(0, q - 2, h0_ready)

            halves(dve, layer0)
            stat(0, NH - 2, h0_ready)
            stat(0, NH - 1, h0_ready)

            def batchnorm(l):
                dve.wait_ge(stl[l], NH)
                link(nc.vector.bn_aggr(agg[:], stats[:].rearrange("p a c -> p (a c)")))
                nc.vector.tensor_scalar(bn_t[:], agg[:, 1:2], EPS, None, ALU.add).then_inc(agg_ok, 1)
                dve.wait_ge(std_ok, l + 1)
                link(nc.vector.reciprocal(bn_std[:], bn_std[:]))
                link(nc.vector.tensor_tensor(bn_a[:, l:l + 1], bn_std[:], vecs[:, 4 + 2 * l:5 + 2 * l], ALU.mult))
                link(nc.vector.tensor_tensor(bn_t[:], agg[:, 0:1], bn_a[:, l:l + 1], ALU.mult))
                nc.vector.tensor_tensor(bn_c[:, l:l + 1], vecs[:, 5 + 2 * l:6 + 2 * l], bn_t[:], ALU.subtract).then_inc(ac_ok, 1)

            for l, W in ((1, W1T), (2, W2T)):
                batchnorm(l - 1)
                dve.wait_ge(bmm_ok, l)
                nc.vector.tensor_scalar(W[:], W[:], bn_a[:, l - 1:l], None, ALU.mult)
                nc.vector.tensor_tensor(bias[:, l:l + 1], ps[:, 7, 0:1], vecs[:, 1 + l:2 + l], ALU.add).then_inc(fold_ok, 1)
                halves(dve, lambda q, s: stat(l, q, hr[l]))
            batchnorm(2)

            def residual(q, s):
                dve.wait_ge(yT_done, q + 1)
                dve.wait_ge(x2_in[s], 16 * (q // PER + 1) if isinstance(q, int) else 16 * ((q - s) // PER + 1))
                pn = np_(q)
                z = zcol(q)[0:pn, :]
                nc.vector.tensor_tensor(z, ps[0:pn, 4 + s % 2, :], z, ALU.add).then_inc(res_ready, 1)

            def ln_stats(q, s):
                pn = np_(q)
                z = zcol(q)
                for j in range(HT):
                    last = nc.vector.bn_stats(lnst[0:pn, s % 2, j, :], z[0:pn, j * D:(j + 1) * D])
                last.then_inc(lnst_ok, 1)

            def ln_moments(q, s):
                dve.wait_ge(lnst_ok, q + 1)
                wait(dve, ln_ready, q - 3)
                pn = np_(q)
                me, mo = lnst[0:pn, s % 2, :, 1], lnst[0:pn, s % 2, :, 4]
                ve, vo = lnst[0:pn, s % 2, :, 2], lnst[0:pn, s % 2, :, 5]
                nmean, var, d, v = (lnm[0:pn, s, k, :] for k in (0, 1, 2, 3))

                def then(ins, k):
                    ins.then_inc(lch, 1)
                    dve.wait_ge(lch, q * 2 + k)

                nc.vector.tensor_tensor(d, me, mo, ALU.subtract)
                nc.vector.tensor_tensor(v, ve, vo, ALU.add)
                then(nc.vector.tensor_tensor(nmean, me, mo, ALU.add), 1)
                nc.vector.scalar_tensor_tensor(out=d, in0=d, scalar=0.25, in1=d, op0=ALU.mult, op1=ALU.mult)
                nc.vector.tensor_scalar(v, v, 1.0 / D, EPS, ALU.mult, ALU.add)
                then(nc.vector.tensor_scalar(nmean, nmean, -0.5, None, ALU.mult), 2)
                nc.vector.tensor_tensor(var, v, d, ALU.add).then_inc(lnv_ok, 1)

            def ln_rstd(q, s, sum_of=None):
                dve.wait_ge(lnsd_ok, q + 1)
                pn = np_(q)
                nc.vector.reciprocal(lnm[0:pn, s, 3, :], lnm[0:pn, s, 2, :]).then_inc(lnrs_ok, 1)
                dve.wait_ge(lnrs_ok, q + 1)
                if sum_of is not None:
                    dve.wait_ge(res_ready, sum_of + 1)
                nc.vector.tensor_tensor(lnm[0:pn, s, 4, :], lnm[0:pn, s, 0, :], lnm[0:pn, s, 3, :], ALU.mult).then_inc(lnr_ok, 1)

            def final(q, s):
                residual(q, s)
                if isinstance(q, int) and q == 0:
                    dve.wait_ge(res_ready, 1)
                else:
                    ln_rstd(q - 1, (s - 1) % PER, sum_of=q)
                ln_stats(q, s)
                ln_moments(q, s)

            halves(dve, final)
            ln_rstd(NH - 1, (NH - 1) % PER)

        @block.tensor
        def _(pe):
            pe.wait_ge(const_ok, 1)
            pe.wait_ge(w_in, 48)
            pe.wait_ge(v_in, 160)
            for k in range(4):
                nc.tensor.transpose(ps[:, 0, k * P:(k + 1) * P], wraw[:, k, :], ident[:])
            nc.tensor.transpose(ps[:, 1, 0:P], wraw[:, 4, :], ident[:])
            nc.tensor.transpose(ps[:, 1, P:P + 10], vraw[:, :], ident[0:10, 0:10]).then_inc(wT_done, 1)
            pe.wait_ge(wT_ready, 1)
            nc.tensor.matmul(ps[:, 2, 0:1], W0cT[:], vecs[:, 0:1], start=True, stop=True).then_inc(b0_done, 1)
            pe.wait_ge(bias_ok, 1)

            def transpose_edges(b, k):
                hf = 2 * b + k
                p = ep(b)
                wait(pe, eT_ready, hf - 1)
                for i in range(HT):
                    c = (k * HT + i) * D
                    last = nc.tensor.transpose(ps[:, 3 + k, i * P:i * P + p], er[0:p, transpose_edges.r, c:c + D], ident[0:p, 0:p])
                last.then_inc(eT_done, 1)

            def project(b, k):
                hf = 2 * b + k
                p = ep(b)
                pe.wait_ge(eT_ready, hf + 1)
                wait(pe, rows_ready, hf - 1)
                for i in range(HT):
                    last = nc.tensor.matmul(ps[0:p, 5 + k, i * D:(i + 1) * D], eT[:, k, i * P:i * P + p], W0bT[:],
                                            start=True, stop=True)
                last.then_inc(pj_done, 1)

            def count(b, r, n):
                p = ep(b)
                pe.wait_ge(e_in[r], 16 * n)
                transpose_edges.r = r
                last_tile = isinstance(b, int) and b == EBF
                for i in range(BI):
                    t = b * BI + i
                    first = isinstance(t, int) and t == 0
                    if i % HT == 0:
                        transpose_edges(b, i // HT)
                    pe.wait_ge(oh_ready, t + 1)
                    nc.tensor.matmul(ps[0:p, i % 2, 0:NT], before[0:p, 0:p], ohh[0:p, i % 4, :],
                                     start=isinstance(t, int) and t < 2, stop=False, skip_group_check=True).then_inc(tri_done, 1)
                    nc.tensor.matmul(ps[:, 2, 0:NT], ohl[0:p, i % 4, :], ohh[0:p, i % 4, :],
                                     start=first, stop=isinstance(t, int) and t == NE - 1, skip_group_check=True)
                    if not first:
                        rest(t - 1, (i - 1) % BI, ep(b) if i else P)
                    if i % HT == HT - 1:
                        project(b, i // HT)

            def rest(t, i, p):
                pe.wait_ge(rank_ready, t + 1)
                nc.tensor.matmul(ps[:, i % 2, 0:NT], notbefore[0:p, :], ohh[0:p, i % 4, :],
                                 start=False, stop=False, skip_group_check=True).then_inc(cmp_done, 1)

            for b in range(4):
                count(b, b, 1)
            with pe.Fori(1, EBF // 4) as it:
                for r in range(4):
                    count(it * 4 + r, r, it + 1)
            for b in range(EBF // 4 * 4, EB):
                count(b, b % 4, b // 4 + 1)
            rest(NE - 1, BI - 1, EPL)

            def xT(q, s):
                pe.wait_ge(x_in[s], 16 * (q // PER + 1) if isinstance(q, int) else 16 * ((q - s) // PER + 1))
                wait(pe, xT_ready, q - 1)
                pn = np_(q)
                for j in range(HT):
                    last = nc.tensor.transpose(ps[:, s % 2, j * P:j * P + pn], xr[0:pn, s, j * D:(j + 1) * D], ident[0:pn, 0:pn])
                last.then_inc(xT_done, 1)

            def mx(q, s):
                pe.wait_ge(xT_ready, q + 1)
                wait(pe, mx_ready, q - 1)
                pn = np_(q)
                for j in range(HT):
                    last = nc.tensor.matmul(ps[0:pn, 2 + s % 2, j * D:(j + 1) * D], stage[:, s % 2, j * P:j * P + pn], W0aT[:],
                                            start=True, stop=True)
                last.then_inc(mx_done, 1)

            def mz(q, s):
                pn = np_(q)
                wait(pe, sum_ready, q - 1)
                for k in range(2):
                    pe.wait_ge(oh0_ready, 2 * q + k + 1)
                    for j in range(2):
                        t = 2 * k + j
                        c = ((s % 2) * HT + t) * RW
                        last = nc.tensor.matmul(ps[0:pn, 4 + s % 2, t * D:(t + 1) * D], oneh[:, k, j, 0:pn],
                                                tabr[:, s // 2, c:c + D], start=True, stop=True)
                    last.then_inc(mz_done, 1)

            def hT(q, s):
                pe.wait_ge(sum_ready, q + 1)
                wait(pe, h0_ready, q - 1)
                pn = np_(q)
                for j in range(HT):
                    last = nc.tensor.transpose(ps[:, 6 + s % 2, j * pn:(j + 1) * pn], xr[0:pn, s, j * D:(j + 1) * D],
                                               ident[0:pn, 0:pn])
                last.then_inc(hT_done, 1)

            pe.wait_ge(rcnt_ok, 1)

            def sums(t, p):
                pe.wait_ge(f_in, 16 * (t + 1))
                nc.tensor.transpose(ps[:, 3, 0:p], f_e[0:p, :], ident[0:p, 0:p]).then_inc(f_T, 1)
                pe.wait_ge(f_Tc, t + 1)
                nc.tensor.matmul(ps[0:p, 5, 0:D], f_eT[:, 0:p], W0bT[:], start=True, stop=True).then_inc(f_P, 1)
                pe.wait_ge(f_keys, t + 1)
                nc.tensor.matmul(ps[0:p, 6, 0:p], f_kb[0:p, 0:p], ident[0:p, 0:p], start=True, stop=True).then_inc(f_row, 1)
                pe.wait_ge(f_Pc, t + 1)
                pe.wait_ge(f_idx, t + 1)
                nc.tensor.matmul(ps[0:p, 7, 0:D], f_same[0:p, 0:p], f_p[0:p, :], start=True, stop=True).then_inc(f_C, 1)

            rebuild(pe, sums)
            xT(0, 0)

            def layer0(q, s):
                if not (isinstance(q, int) and q == NH - 1):
                    xT(q + 1, (s + 1) % PER)
                mx(q, s)
                mz(q, s)
                if not (isinstance(q, int) and q == 0):
                    hT(q - 1, (s - 1) % PER)

            halves(pe, layer0)
            hT(NH - 1, (NH - 1) % PER)

            for l, W in ((1, W1T), (2, W2T)):
                pe.wait_ge(ac_ok, l)
                nc.tensor.matmul(ps[:, 7, 0:1], W[:], bn_c[:, l - 1:l], start=True, stop=True).then_inc(bmm_ok, 1)
                pe.wait_ge(fold_ok, l)

                def layer(q, s):
                    wait(pe, hr[l], q - 3)
                    pn = np_(q)
                    nc.tensor.matmul(ps[:, s, 0:HT * pn], W[:], hcol(q), start=True, stop=True).then_inc(mm[l], 1)

                halves(pe, layer)

            def yT(q, s):
                pe.wait_ge(y_ready, q + 1)
                wait(pe, res_ready, q - 1)
                pn = np_(q)
                for j in range(HT):
                    last = nc.tensor.transpose(ps[0:pn, 4 + s % 2, j * P:(j + 1) * P], stage[:, s % 2, j * pn:(j + 1) * pn], ident[:])
                last.then_inc(yT_done, 1)

            halves(pe, yT)


_USED = ["x", "src", "edge_attr_128", "L0_gnn_u", "L0_gnn_W0", "L0_gnn_b0", "L0_gnn_W1", "L0_gnn_b1", "L0_gnn_W2", "L0_gnn_b2",
         "L0_gnn_g0", "L0_gnn_bt0", "L0_gnn_g1", "L0_gnn_bt1", "L0_gnn_g2", "L0_gnn_bt2"]


def kernel(**inputs):
    import numpy as _np
    import concourse.bacc as _bacc
    from concourse import mybir as _mybir
    from concourse.bass_utils import run_bass_kernel_spmd as _run

    nc = _bacc.Bacc("TRN2", target_bir_lowering=False, num_devices=1, dynamic_dma_scratch_size=2048)
    arrays, args = {}, []
    for name in _USED:
        a = _np.ascontiguousarray(inputs[name])
        arrays[f"in_{name}"] = a
        args.append(nc.dram_tensor(f"in_{name}", a.shape, _mybir.dt.from_np(a.dtype), kind="ExternalInput").ap())
    n = inputs["x"].shape[0]
    tiles = (n + 1023) // 1024 * 8
    table = nc.dram_tensor("edge_table", (128 * tiles + 128 * ((inputs["src"].shape[0] + 1023) // 1024 * 8), 129), _mybir.dt.float32, kind="Internal").ap()
    out = nc.dram_tensor("out", inputs["x"].shape, _mybir.dt.float32, kind="ExternalOutput").ap()
    gnn_resnorm_kernel(nc, *args, table, out)
    r = _run(nc, [arrays], core_ids=[0])
    return r.results[0]["out"]
```

```python
import concourse.bass as bass
from concourse import mybir
from contextlib import ExitStack


def gnn_resnorm_kernel(nc, x, src, edge_attr, u, W0, b0, W1, b1, W2, b2, g0, bt0, g1, bt1, g2, bt2, table, out):
    fp32, bf16, fp16, i32 = mybir.dt.float32, mybir.dt.bfloat16, mybir.dt.float16, mybir.dt.int32
    ALU = mybir.AluOpType
    ACT = mybir.ActivationFunctionType
    AX = mybir.AxisListType.X

    N, D = x.shape
    E = edge_attr.shape[0]
    P = 128
    BI = 8
    BN = P * BI
    NBF = N // BN
    PL = (N - NBF * BN) // BI
    NB = NBF + 1
    NT = NB * BI
    HT = 4
    HC = HT * P
    NH = 2 * NB
    NHF = 2 * NBF
    EBF = E // BN
    ET = EBF * BI
    EPL = (E - EBF * BN) // BI
    EB = EBF + 1
    NE = EB * BI
    RW = D + 1
    SLOTS = P * NT
    ZT = 14
    NZ = NT // ZT
    EPS = 1e-5
    BEHIND = 7
    BANKS = 8
    PER = 4
    RING = 4
    LAG = 8
    LATE = 4
    XH = EBF - LAG + LATE * LAG
    assert N % BI == 0 and E % BI == 0 and NT % ZT == 0 and NHF % BANKS == 0 and 0 < PL < P and 0 < EPL < P
    assert EBF % RING == 0 and LAG % RING == 0 and LATE == 4
    assert XH == NBF and NBF % PER == 0

    x_full = x[0:NBF * BN, :].rearrange("(g p s i) f -> p s g (i f)", p=P, s=2, i=HT)
    x_last = x[NBF * BN:N, :].rearrange("(p s i) f -> p s (i f)", s=2, i=HT)
    o_full = out[0:NBF * BN, :].rearrange("(g p s i) f -> p s g (i f)", p=P, s=2, i=HT)
    o_last = out[NBF * BN:N, :].rearrange("(p s i) f -> p s (i f)", s=2, i=HT)
    e_full = edge_attr[0:EBF * BN, :].rearrange("(p t) f -> p (t f)", p=P)
    e_last = edge_attr[EBF * BN:E, :].rearrange("(p t) f -> p (t f)", t=BI)
    src_full = src[0:EBF * BN].rearrange("(p t) -> p t", p=P)
    src_last = src[EBF * BN:E].rearrange("(p t) -> p t", t=BI)
    tab = table[0:SLOTS, :].rearrange("(p j) c -> p (j c)", p=P)

    ctx = ExitStack()
    with ctx:
        def sb(name, shape, dt=fp32, where=ctx):
            return where.enter_context(nc.sbuf_tensor(name, shape, dt))

        def sem(name):
            return ctx.enter_context(nc.semaphore(name))

        ident = sb("ident", [P, P])
        lo1_row = sb("lo1_row", [P, P])
        W0aT = sb("W0aT", [P, P])
        vecs = sb("vecs", [P, 10])
        rcnt = sb("rcnt", [P, NT])
        stats = sb("stats", [P, NH, 6])
        agg = sb("agg", [P, 2])
        eps = sb("eps", [P, 1])
        bn_std = sb("bn_std", [P, 1])
        bn_a = sb("bn_a", [P, 3])
        bn_c = sb("bn_c", [P, 3])
        bn_t = sb("bn_t", [P, 1])
        bias = sb("bias", [P, 3])
        ovf = sb("ovf", [P, 1], i32)
        xr = sb("xr", [P, 4, HC])
        tabr = sb("tabr", [P, PER, HT * RW])
        stage = sb("stage", [P, 2, HC])
        oneh = sb("oneh", [P, 2, HC])
        h_last = tabr[:, 2:4, :].rearrange("p a c -> p (a c)")[:, 0:BI * PL]
        W1T, W2T = oneh[:, 0, 0:P], oneh[:, 0, P:2 * P]
        lnst = oneh[:, 1, 0:4 * HT * 6].rearrange("p (a i c) -> p a i c", a=2, i=2 * HT)
        lnm = oneh[:, 1, P:P + 4 * 5 * 2 * HT].rearrange("p (a k i) -> p a k i", a=4, k=5)

        ps = ctx.enter_context(nc.psum_tensor("ps", [P, 8, 512], fp32))

        sa = ExitStack()
        with sa:
            rows = sb("rows", [P, RING, BI, RW], where=sa)
            er = sb("er", [P, 4, BI * D], where=sa)
            hi_row = sb("hi_row", [P, NT], fp16, sa)
            iot = sb("iot", [P, NT], i32, sa)
            pidx_i = sb("pidx_i", [P, 1], i32, sa)
            pidx = sb("pidx", [P, 1], fp32, sa)
            lo_row = sb("lo_row", [P, P], fp16, sa)
            ohh = sb("ohh", [P, 4, NT], bf16, sa)
            ohl = sb("ohl", [P, 4, P], bf16, sa)
            junk = sb("junk", [P, 2, NT], bf16, sa)
            before = sb("before", [P, P], bf16, sa)
            notbefore = sb("notbefore", [P, P], bf16, sa)
            srcI = sb("srcI", [P, NE], i32, sa)
            t1 = sb("t1", [P, NE], i32, sa)
            t2 = sb("t2", [P, NE], i32, sa)
            t3 = sb("t3", [P, NE], i32, sa)
            hiF = sb("hiF", [P, NE], fp32, sa)
            loF = sb("loF", [P, NE], fp32, sa)
            lo1F = sb("lo1F", [P, NE], fp32, sa)
            rank = sb("rank", [P, 2, BI], fp32, sa)
            slot0 = sb("slot0", [P, NE], fp32, sa)
            dump_i = sb("dump_i", [P, NE], i32, sa)
            dump = sb("dump", [P, NE], fp32, sa)
            posf = sb("posf", [P, 3, BI], fp32, sa)
            posI = sb("posI", [P, NE], i32, sa)
            zero = sb("zero", [P, ZT * RW], fp32, sa)
            wraw = sb("wraw", [P, 3, P], fp32, sa)
            vraw = sb("vraw", [10, P], fp32, sa)
            W0bT = sb("W0bT", [P, P], fp32, sa)
            W0cT = sb("W0cT", [P, P], fp32, sa)
            tot = sb("tot", [P, NT], fp32, sa)
            xT_b = sb("xT_b", [P, HC], fp32, sa)
            tmax = sb("tmax", [P, 1], fp32, sa)
            f_e = sb("f_e", [P, D], fp32, sa)
            f_eT = sb("f_eT", [P, P], fp32, sa)
            f_p = sb("f_p", [P, D], fp32, sa)
            f_key = sb("f_key", [P, 4], fp32, sa)
            f_get = sb("f_get", [P, 1], i32, sa)
            f_put = sb("f_put", [P, 1], i32, sa)
            f_kb = sb("f_kb", [P, P], fp32, sa)
            f_same = sb("f_same", [P, P], fp32, sa)
            f_earlier = sb("f_earlier", [P, P], fp32, sa)
            f_junk = sb("f_junk", [P, P], fp32, sa)
            f_old = sb("f_old", [P, RW], fp32, sa)
            f_new = sb("f_new", [P, RW], fp32, sa)
        h = sb("h", [P, NHF * HC])

        xT_places = (stage[:, 1, :], xT_b[:])

        w_in, v_in, src_in, zero_done = (
            sem("w_in"), sem("v_in"), sem("src_in"), sem("zero_done"))
        scat_done = [sem(f"scat_done{i}") for i in range(RING)]
        e_in = [sem(f"e_in{i}") for i in range(4)]
        px_in = [sem(f"px_in{i}") for i in range(4)]
        px_T, px_Tc, px_M, px_Mc, lo1_ok = sem("px_T"), sem("px_Tc"), sem("px_M"), sem("px_Mc"), sem("lo1_ok")
        zc_ready, sum2_ready = sem("zc_ready"), sem("sum2_ready")
        x_in = [sem(f"x_in{i}") for i in range(4)]
        x2_in = [sem(f"x2_in{i}") for i in range(4)]
        tab_in = [sem(f"tab_in{i}") for i in range(4)]
        w12_in, w12T_done, w12_ok = sem("w12_in"), sem("w12T_done"), sem("w12_ok")
        out_w = [sem(f"out_w{i}") for i in range(4)]
        iota_ok, zero_ok, const_ok, srcset = (
            sem("iota_ok"), sem("zero_ok"), sem("const_ok"), sem("srcset"))
        wT_done, wT_ready, b0_done, bias_ok = sem("wT_done"), sem("wT_ready"), sem("b0_done"), sem("bias_ok")
        oh_ready, tri_done, rank_ready, cmp_done, pos_ready = (
            sem("oh_ready"), sem("tri_done"), sem("rank_ready"), sem("cmp_done"), sem("pos_ready"))
        eT_done, eT_ready, pj_done, rows_ready = sem("eT_done"), sem("eT_ready"), sem("pj_done"), sem("rows_ready")
        dve_s, ovf_ok, rcnt_ok = sem("dve_s"), sem("ovf_ok"), sem("rcnt_ok")
        turn = sem("turn")
        act_turn = sem("act_turn")
        xT_done, xT_ready, mx_done, oh0_ready, mz_done, mx_ready, sum_ready, hT_done, h0_ready, st0 = (
            sem("xT_done"), sem("xT_ready"), sem("mx_done"), sem("oh0_ready"), sem("mz_done"), sem("mx_ready"),
            sem("sum_ready"), sem("hT_done"), sem("h0_ready"), sem("st0"))
        f_zero, f_in, f_got, f_done = sem("f_zero"), sem("f_in"), sem("f_got"), sem("f_done")
        f_T, f_Tc, f_P, f_Pc, f_keys, f_row, f_idx, f_C, f_sum, fch = (
            sem("f_T"), sem("f_Tc"), sem("f_P"), sem("f_Pc"), sem("f_keys"), sem("f_row"), sem("f_idx"), sem("f_C"),
            sem("f_sum"), sem("fch"))
        f_sameok = sem("f_sameok")
        lna_ready, lnv_ready = sem("lna_ready"), sem("lnv_ready")
        lnrs_ok, lnm1_ok, lnm2_ok, lnm3_ok = sem("lnrs_ok"), sem("lnm1_ok"), sem("lnm2_ok"), sem("lnm3_ok")
        eps_ok = sem("eps_ok")
        mm = [None, sem("mm1"), sem("mm2")]
        hr = [None, sem("hr1"), sem("hr2")]
        stl = [st0, sem("st1"), sem("st2")]
        agg_ok, std_ok, fold_ok, bmm_ok, ac_ok = (
            sem("agg_ok"), sem("std_ok"), sem("fold_ok"), sem("bmm_ok"), sem("ac_ok"))
        y_ready, sum_done, res_ready, lnst_ok, lnv_ok, lnsd_ok, lnr_ok = (
            sem("y_ready"), sem("sum_done"), sem("res_ready"), sem("lnst_ok"), sem("lnv_ok"), sem("lnsd_ok"),
            sem("lnr_ok"))

        def wait(eng, s, n):
            if not (isinstance(n, int) and n <= 0):
                eng.wait_ge(s, n)

        def np_(q):
            return PL if isinstance(q, int) and q >= NHF else P

        def hcol(q):
            if isinstance(q, int) and q >= NHF:
                return h_last[:, (q - NHF) * HT * PL:(q - NHF + 1) * HT * PL]
            return h[:, bass.ds(q * HC, HC)] if not isinstance(q, int) else h[:, q * HC:(q + 1) * HC]

        def half_of(t, s):
            if isinstance(t, int):
                return t if t >= NHF else t // 2 + t % 2 * NBF
            return (t - s % 2) // 2 + s % 2 * NBF

        def has_x(t, s):
            return s % 2 == 0 or (isinstance(t, int) and t >= NHF)

        def xnum(t):
            return NBF + t - NHF if isinstance(t, int) and t >= NHF else t // 2

        def x_after(t, k):
            return t + k if not isinstance(t, int) or t + k <= NHF else NHF + (t + k - NHF) // 2

        def wait_x(eng, s_, t):
            wait(eng, s_, xnum(t) - 1 if isinstance(t, int) else (t - 2) // 2)

        def xplace(t, s):
            return xnum(t) % 2 if isinstance(t, int) else s // 2

        def part(t, s):
            return xr[:, xplace(t, s), :] if isinstance(t, int) and t >= NHF else hcol(half_of(t, s))

        def total(s):
            return xr[:, 2 + s % 2, :]

        def zcol(q):
            if isinstance(q, int):
                return xr[:, q, :] if q < PER else h[:, (q - PER) * HC:(q - PER + 1) * HC]
            return h[:, bass.ds((q - PER) * HC, HC)]

        def halves(eng, step, peel=1, per=PER):
            for q in range(peel * per):
                step(q, q % per)
            with eng.Fori(peel, NHF // per - 1) as it:
                for s in range(per):
                    step(it * per + s, s)
            for q in range(NHF - per, NH):
                step(q, q % per)

        def dve_adds(s):
            return s % PER == 3

        def pair(q, s):
            return (q - s % 2) // 2

        def applied(eng, q):
            q, odd = q
            if not (isinstance(q, int) and q < 0):
                eng.wait_ge(lnv_ready if odd else lna_ready, (q - odd) // 2 + 1)

        def quads(eng, step, b0, b1):
            lo, hi = b0 // RING + 1, (b1 - 1) // RING
            for b in range(b0, min(lo * RING, b1)):
                step(b, b % RING)
            if hi > lo:
                with eng.Fori(lo, hi) as it:
                    for r_ in range(RING):
                        step(it * RING + r_, r_)
            for b in range(max(lo, hi) * RING, b1):
                step(b, b % RING)

        def late_x(b, r_, m):
            return b * LATE + (EBF - LAG - 1 - LATE * EBF + m), (m - 1) % PER

        def ep(b):
            return EPL if isinstance(b, int) and b == EBF else P

        def rebuild(eng, step):
            eng.wait_ge(ovf_ok, 1)
            full = eng.value_load(ovf[0:1, 0:1], min_val=0, max_val=1)
            with eng.If(full):
                with eng.Fori(0, ET) as t:
                    step(t, P)
                for t in range(ET, NE):
                    step(t, EPL)
                eng.wait_ge(f_done, 16 * NE)

        block = ctx.enter_context(nc.Block())

        @block.sync
        def _(sp):
            sp.wait_ge(srcset, 1)
            sp.dma_start(srcI[:, 0:ET], src_full).then_inc(src_in, 16)
            sp.dma_start(srcI[0:EPL, ET:NE], src_last).then_inc(src_in, 16)
            sp.dma_start(wraw[:, 0:3, :].rearrange("p a b -> p (a b)"), W0).then_inc(w_in, 16)
            for k, v in enumerate((None, b0, b1, b2, g0, bt0, g1, bt1, g2, bt2)):
                sp.dma_start(vraw[k:k + 1, :], u[0:1, :] if k == 0 else v.rearrange("(a b) -> a b", a=1)).then_inc(v_in, 16)

            def load_edges(b, r):
                wait(sp, eT_done, 2 * (b - 3))
                if isinstance(b, int) and b == EBF:
                    sp.dma_start(er[0:EPL, r, :], e_last).then_inc(e_in[r], 16)
                else:
                    cols = (slice(b * BN, (b + 1) * BN) if isinstance(b, int) else bass.ds(b * BN, BN))
                    sp.dma_start(er[:, r, :], e_full[:, cols]).then_inc(e_in[r], 16)

            def load_px(i, s):
                wait(sp, px_T, i - 3)
                if isinstance(i, int):
                    sp.dma_start(xr[:, s, :], x_full[:, 1, i, :]).then_inc(px_in[s], 16)
                else:
                    sp.dma_start(xr[:, s, :], x_full[:, 1, bass.ds(i, 1), :]).then_inc(px_in[s], 16)

            for b in range(RING):
                load_edges(b, b)
            sp.wait_ge(zero_done, 16 * NZ)
            for i in range(RING):
                load_px(i, i)

            def feed(b, r_):
                load_edges(b - (LAG - RING), r_)
                if not (isinstance(b, int) and b == LAG):
                    load_px(b - (LAG + 1 - PER), (r_ - 1) % PER)

            quads(sp, feed, LAG, EBF)
            for b in range(EBF, EB + LAG):
                i0 = late_x(b, b % RING, 0)[0] + PER
                for i in range(i0, min(i0 + LATE, XH)):
                    load_px(i, i % PER)
                if b - (LAG - RING) < EB:
                    load_edges(b - (LAG - RING), b % RING)

            def load_x(t, s):
                wait_x(sp, xT_done, t)
                i = xplace(t, s)
                if isinstance(t, int) and t >= NHF:
                    sp.dma_start(xr[0:PL, i, :], x_last[:, t % 2, :]).then_inc(x_in[i], 16)
                else:
                    g = slice(t // 2, t // 2 + 1) if isinstance(t, int) else bass.ds(t // 2, 1)
                    sp.dma_start(xr[:, i, :], x_full[:, 0, g, :]).then_inc(x_in[i], 16)

            def load_table(t, s):
                wait(sp, mz_done, t - 3)
                n, q = HT * RW, half_of(t, s)
                cols = slice(q * n, (q + 1) * n) if isinstance(q, int) else bass.ds(q * n, n)
                sp.dma_start(tabr[:, s, :], tab[:, cols]).then_inc(tab_in[s], 16)

            sp.wait_ge(px_T, XH)
            for t in (0, 2):
                load_x(t, t)
            for r_ in range(RING):
                sp.wait_ge(scat_done[r_], 16 * BI * len(range(r_, EB, RING)))

            def fetch(t, p):
                wait(sp, f_done, 16 * t)
                v = e_last[:, (t - ET) * D:(t - ET + 1) * D] if isinstance(t, int) else e_full[:, bass.ds(t * D, D)]
                sp.dma_start(f_e[0:p, :], v).then_inc(f_in, 16)

            rebuild(sp, fetch)
            sp.wait_ge(px_Mc, XH)
            sp.wait_ge(rcnt_ok, 1)
            for t in range(PER):
                load_table(t, t)
            load_x(PER, 0)
            with sp.Fori(1, NHF // PER - 1) as it:
                for s in range(PER):
                    load_table(it * PER + s, s)
                    if s % 2 == 0:
                        load_x(it * PER + s + 2, (s + 2) % PER)
            for t in range(NHF - PER, NH):
                load_table(t, t % PER)
                if t % 2 == 0 and t < NHF + 1:
                    load_x(x_after(t, 2), x_after(t, 2) % PER)
            sp.wait_ge(mz_done, NHF + 1)
            sp.dma_start(tabr[:, 0, 0:P], W1).then_inc(w12_in, 16)
            sp.dma_start(tabr[:, 0, P:2 * P], W2).then_inc(w12_in, 16)

            def rows_of(full, last, q, k):
                if isinstance(q, int):
                    return last[:, q % 2, :] if q >= NHF else full[:, q // NBF, q % NBF, :]
                return full[:, k, bass.ds(q - k * NBF, 1), :]

            def load_x2(q, s, k=None):
                if not dve_adds(s):
                    wait(sp, sum_done, q - 3)
                elif not (isinstance(q, int) and q < PER):
                    sp.wait_ge(res_ready, (q - 3) // PER)
                sp.dma_start(zcol(q)[0:np_(q), :], rows_of(x_full, x_last, q, k)).then_inc(x2_in[s], 16)

            def store(q, s, k=None):
                applied(sp, (q, s % 2))
                sp.dma_start(rows_of(o_full, o_last, q, k), zcol(q)[0:np_(q), :]).then_inc(out_w[s], 16)

            sp.wait_ge(hT_done, NH)
            for q in range(PER):
                load_x2(q, q)

            def move(q, s, k=None):
                if not (isinstance(q, int) and q + PER >= NH):
                    load_x2(q + PER, s, k)
                if not (isinstance(q, int) and q < BEHIND):
                    store(q - BEHIND, (s - BEHIND) % PER, k)

            for k in range(2):
                for q in range(k * NBF, k * NBF + 3 * PER):
                    move(q, q % PER)
                with sp.Fori(k * NBF // PER + 3, (k + 1) * NBF // PER - 1) as it:
                    for s in range(PER):
                        move(it * PER + s, s, k)
                for q in range((k + 1) * NBF - PER, (k + 1) * NBF):
                    move(q, q % PER)
            for q in range(NHF, NH + BEHIND):
                if q < NH:
                    move(q, q % PER)
                else:
                    store(q - BEHIND, (q - BEHIND) % PER)
            for s in range(PER):
                sp.wait_ge(out_w[s], 16 * len(range(s, NH, PER)))

        @block.gpsimd
        def _(pool):
            nc.gpsimd.memset(srcI[:, ET:NE], 0).then_inc(srcset, 1)
            nc.gpsimd.memset(zero[:], 0.0).then_inc(zero_ok, 1)
            nc.gpsimd.iota(iot[:], [[1, NT]], base=0, channel_multiplier=0).then_inc(iota_ok, 1)
            nc.gpsimd.iota(pidx_i[:], [[0, 1]], base=0, channel_multiplier=1).then_inc(iota_ok, 1)
            nc.gpsimd.iota(dump_i[:], [[P, NE]], base=SLOTS, channel_multiplier=1).then_inc(iota_ok, 1)
            pool.wait_ge(zero_ok, 1)
            for z in range(NZ):
                pool.dma_start(tab[:, z * ZT * RW:(z + 1) * ZT * RW], zero[:]).then_inc(zero_done, 16)
            pool.wait_ge(zero_done, 16 * NZ)

            for b in range(EB):
                pool.wait_ge(pos_ready, b + 1)
                pool.wait_ge(rows_ready, 2 * (b + 1))
                p, r_ = ep(b), b % RING
                for i in range(BI):
                    t = b * BI + i
                    pool.indirect_dma_start(
                        out=table[:, :], out_offset=bass.IndirectOffsetOnAxis(ap=posI[0:p, t:t + 1], axis=0),
                        in_=rows[0:p, r_, i, :], in_offset=None).then_inc(scat_done[r_], 16)

            def gather_scatter(t, p):
                pool.wait_ge(f_zero, 16 * NZ)
                wait(pool, f_done, 16 * t)
                pool.wait_ge(f_idx, t + 1)
                pool.sem_inc(turn, 1)
                pool.indirect_dma_start(out=f_old[0:p, :], out_offset=None, in_=table[0:SLOTS, :],
                                        in_offset=bass.IndirectOffsetOnAxis(ap=f_get[0:p, 0:1], axis=0)).then_inc(f_got, 16)
                pool.wait_ge(f_sum, t + 1)
                pool.sem_inc(turn, 1)
                pool.indirect_dma_start(out=table[:, :], out_offset=bass.IndirectOffsetOnAxis(ap=f_put[0:p, 0:1], axis=0),
                                        in_=f_new[0:p, :], in_offset=None).then_inc(f_done, 16)

            pool.wait_ge(ovf_ok, 1)
            with pool.If(pool.value_load(ovf[0:1, 0:1], min_val=0, max_val=1)):
                for r_ in range(RING):
                    pool.wait_ge(scat_done[r_], 16 * BI * len(range(r_, EB, RING)))
                for z in range(NZ):
                    pool.dma_start(tab[:, z * ZT * RW:(z + 1) * ZT * RW], zero[:]).then_inc(f_zero, 16)
            rebuild(pool, gather_scatter)


            def add0(t, s):
                pool.wait_ge(zc_ready, (t - 1) // 2 + 1)
                pool.sem_inc(turn, 1)
                v = total(s)
                nc.gpsimd.tensor_tensor(v, part(t, s), v, ALU.add).then_inc(sum2_ready, 1)

            pool.wait_ge(px_Mc, XH)
            halves(pool, lambda t, s: None if has_x(t, s) else add0(t, s))

            def moments(k, r, last):
                pn = PL if last else P
                me, mo = lnst[0:pn, r % 2, :, 1], lnst[0:pn, r % 2, :, 4]
                ve, vo = lnst[0:pn, r % 2, :, 2], lnst[0:pn, r % 2, :, 5]
                nmean, v, d = (lnm[0:pn, r, i, :] for i in range(3))
                pool.wait_ge(lnst_ok, 2 * k + 2)
                applied(pool, (2 * k - BANKS, 0))
                applied(pool, (2 * k - BANKS + 1, 1))
                pool.sem_inc(turn, 1)
                nc.gpsimd.tensor_tensor(d, me, mo, ALU.subtract)
                nc.gpsimd.tensor_tensor(v, ve, vo, ALU.add)
                nc.gpsimd.tensor_tensor(nmean, me, mo, ALU.add).then_inc(lnm1_ok, 1)
                pool.wait_ge(lnm1_ok, k + 1)
                pool.sem_inc(turn, 1)
                nc.gpsimd.tensor_tensor(d, d, d, ALU.mult)
                nc.gpsimd.tensor_scalar(nmean, nmean, -0.5, None, ALU.mult).then_inc(lnm2_ok, 1)
                pool.wait_ge(lnm2_ok, k + 1)
                pool.sem_inc(turn, 1)
                nc.gpsimd.tensor_scalar(d, d, D / 4.0, None, ALU.mult).then_inc(lnm3_ok, 1)
                pool.wait_ge(lnm3_ok, k + 1)
                pool.sem_inc(turn, 1)
                nc.gpsimd.tensor_tensor(v, v, d, ALU.add).then_inc(lnv_ok, 1)

            def shift(k, r, last):
                pn = PL if last else P
                pool.wait_ge(lnrs_ok, k + 1)
                pool.sem_inc(turn, 1)
                nc.gpsimd.tensor_tensor(lnm[0:pn, r, 4, :], lnm[0:pn, r, 0, :], lnm[0:pn, r, 3, :], ALU.mult).then_inc(lnr_ok, 1)

            def pairs(k, r):
                if not (isinstance(k, int) and k == 0):
                    shift(k - 1, (r - 1) % 4, False)
                moments(k, r, isinstance(k, int) and k == NBF)

            for k in range(4):
                pairs(k, k)
            with pool.Fori(1, NBF // 4) as it:
                for r in range(4):
                    pairs(it * 4 + r, r)
            pairs(NBF, NBF % 4)
            shift(NBF, NBF % 4, True)

        @block.scalar
        def _(act):
            def e_T(b, k):
                hf = 2 * b + k
                p = ep(b)
                act.wait_ge(eT_done, hf + 1)
                wait(act, pj_done, hf)
                nc.scalar.activation(stage[:, 0, :].rearrange("f (i e) -> f i e", i=HT)[:, :, 0:p],
                                     ps[:, 3, :].rearrange("f (i e) -> f i e", i=HT)[:, :, 0:p],
                                     ACT.Copy).then_inc(eT_ready, 1)

            def e_P(b, r_, k):
                hf = 2 * b + k
                p = ep(b)
                if k == 0:
                    if not (isinstance(b, int) and b < RING):
                        act.wait_ge(scat_done[r_], 16 * BI * (b // RING) if isinstance(b, int) else (16 * BI // RING) * (b - r_))
                    lo1 = lo1F[0:p, b * BI:(b + 1) * BI] if isinstance(b, int) else lo1F[:, bass.ds(b * BI, BI)]
                    nc.scalar.activation(rows[0:p, r_, :, D], lo1, ACT.Copy)
                act.wait_ge(pj_done, hf + 1)
                nc.scalar.activation(rows[0:p, r_, k * HT:(k + 1) * HT, 0:D], ps[0:p, 5, :].rearrange("e (i f) -> e i f", i=HT),
                                     ACT.Copy).then_inc(rows_ready, 1)

            def x_T(i, s):
                act.wait_ge(px_T, i + 1)
                wait(act, px_M, i - 1)
                nc.scalar.activation(xT_places[s % 2], ps[:, 4 + 3 * (s % 2), :], ACT.Copy).then_inc(px_Tc, 1)

            def x_P(i):
                act.wait_ge(px_M, i + 1)
                nc.scalar.activation(hcol(i + NBF), ps[:, 6, :], ACT.Copy).then_inc(px_Mc, 1)

            def middle(b, r_):
                with_x = not (isinstance(b, int) and b == LAG)
                e_T(b - LAG, 0)
                if with_x:
                    x_T(b - (LAG + 1), r_ - 1)
                e_P(b - LAG, r_, 0)
                e_T(b - LAG, 1)
                if with_x:
                    x_P(b - (LAG + 1))
                e_P(b - LAG, r_, 1)

            def late(b, r_, with_x=True):
                before_x, xs = late_x(b, r_, -1), [late_x(b, r_, m) for m in range(LATE)]
                e_T(b - LAG, 0)
                if not (isinstance(b, int) and b == EBF):
                    x_P(before_x[0])
                x_T(*xs[0])
                e_P(b - LAG, r_, 0)
                if with_x:
                    x_T(*xs[1])
                x_P(xs[0][0])
                e_T(b - LAG, 1)
                if with_x:
                    x_P(xs[1][0])
                    x_T(*xs[2])
                e_P(b - LAG, r_, 1)
                if with_x:
                    x_T(*xs[3])
                    x_P(xs[2][0])

            act.wait_ge(lo1_ok, 1)
            quads(act, middle, LAG, EBF)
            quads(act, late, EBF, EB + LAG - 1)
            late(EB + LAG - 1, (EB + LAG - 1) % RING, with_x=False)

            def copies(t, p):
                act.wait_ge(f_T, t + 1)
                nc.scalar.activation(f_eT[:, 0:p], ps[:, 3, 0:p], ACT.Copy).then_inc(f_Tc, 1)
                act.wait_ge(f_P, t + 1)
                nc.scalar.activation(f_p[0:p, :], ps[0:p, 5, 0:D], ACT.Copy).then_inc(f_Pc, 1)

            rebuild(act, copies)

            def copy_xT(t, s):
                act.wait_ge(xT_done, xnum(t) + 1)
                wait_x(act, mx_done, t)
                pn, i = np_(t), xplace(t, s)
                nc.scalar.activation(stage[:, i, :].rearrange("f (i e) -> f i e", i=HT)[:, :, 0:pn],
                                     ps[:, i, :].rearrange("f (i e) -> f i e", i=HT)[:, :, 0:pn],
                                     ACT.Copy).then_inc(xT_ready, 1)

            def copy_mx(t, s):
                act.wait_ge(mx_done, xnum(t) + 1)
                if not isinstance(t, int):
                    act.sem_inc(act_turn, 1)
                pn = np_(t)
                nc.scalar.activation(part(t, s)[0:pn, :], ps[0:pn, 2 + xplace(t, s), :], ACT.Copy).then_inc(mx_ready, 1)

            def relu0(t, s):
                act.wait_ge(hT_done, t + 1)
                if not isinstance(t, int):
                    act.sem_inc(act_turn, 1)
                pn = np_(t)
                nc.scalar.activation(hcol(half_of(t, s)), ps[:, 6 + s % 2, 0:HT * pn], ACT.Relu,
                                     bias=bias[:, 0:1]).then_inc(h0_ready, 1)

            def mean0(t, s):
                act.wait_ge(mz_done, t + 1)
                wait(act, hT_done, t - 1)
                if not isinstance(t, int):
                    act.sem_inc(act_turn, 1)
                for j in range(HT):
                    c, i = slice(j * D, (j + 1) * D), half_of(t, s) * HT + j
                    last = nc.scalar.activation(total(s)[:, c], ps[:, 4 + s % 2, c], ACT.Copy,
                                                scale=rcnt[:, i:i + 1] if isinstance(i, int) else rcnt[:, bass.ds(i, 1)])
                last.then_inc(zc_ready, 1)

            act.wait_ge(bias_ok, 1)
            act.wait_ge(rcnt_ok, 1)
            copy_xT(0, 0)
            copy_xT(2, 2)
            act.wait_ge(tab_in[0], 16)
            copy_mx(0, 0)

            def layer0(t, s):
                some = lambda k: not (isinstance(t, int) and (t < k or t - k >= NH))
                if some(3):
                    relu0(t - 3, (s - 3) % PER)
                if s % 2 and some(-1):
                    copy_xT(x_after(t, 3), (s + 3) % PER)
                if s % 2 == 0 and some(-1):
                    copy_mx(x_after(t, 2), (s + 2) % PER)
                if some(0) and not has_x(t, s):
                    mean0(t, s)

            halves(act, layer0)
            for t in range(NH, NH + 3):
                layer0(t, t % PER)

            def bn_sqrt(l):
                act.wait_ge(agg_ok, l + 1)
                nc.scalar.activation(bn_std[:], bn_t[:], ACT.Sqrt).then_inc(std_ok, 1)

            bn_sqrt(0)
            for l in (1, 2):
                act.wait_ge(fold_ok, l)

                def layer(q, s):
                    act.wait_ge(mm[l], q + 1)
                    pn = np_(q)
                    nc.scalar.activation(hcol(q), ps[:, s, 0:HT * pn], ACT.Relu, bias=bias[:, l:l + 1]).then_inc(hr[l], 1)

                halves(act, layer)
                bn_sqrt(l)

            act.wait_ge(ac_ok, 3)
            act.wait_ge(eps_ok, 1)

            def normalise(q, s):
                wait(act, sum_done, q - 1)
                pn = np_(q)
                nc.scalar.activation(stage[:, s % 2, 0:HT * pn], hcol(q), ACT.Identity,
                                     bias=bn_c[:, 2:3], scale=bn_a[:, 2:3]).then_inc(y_ready, 1)

            def ln_sqrt(q, s):
                act.wait_ge(lnv_ok, pair(q, s) + 1)
                pn, r = np_(q), s // 2
                nc.scalar.activation(lnm[0:pn, r, 2, :], lnm[0:pn, r, 1, :], ACT.Sqrt, bias=eps[0:pn, 0:1],
                                     scale=1.0 / D).then_inc(lnsd_ok, 1)

            def ln_apply(q, s):
                act.wait_ge(lnr_ok, pair(q, s) + 1)
                pn, r = np_(q), s // 2
                for j in range(HT):
                    c, i = slice(j * D, (j + 1) * D), s % 2 * HT + j
                    last = nc.scalar.activation(zcol(q)[0:pn, c], ps[0:pn, s, c], ACT.Identity,
                                                bias=lnm[0:pn, r, 4, i:i + 1], scale=lnm[0:pn, r, 3, i:i + 1])
                last.then_inc(lna_ready, 1)

            normalise(0, 0)

            def final(q, s):
                some = lambda k: not (isinstance(q, int) and (q < k or q - k >= NH))
                if s % 2 and some(5):
                    ln_sqrt(q - 5, (s - 5) % BANKS)
                if some(-1):
                    normalise(q + 1, (s + 1) % BANKS)
                if s % 2 == 0 and some(6):
                    ln_apply(q - 6, (s - 6) % BANKS)

            halves(act, final, peel=2, per=BANKS)
            for q in range(NH, NH + 6):
                final(q, q % BANKS)

        @block.vector
        def _(dve):
            chain = [0]

            def link(ins):
                chain[0] += 1
                ins.then_inc(dve_s, 1)
                dve.wait_ge(dve_s, chain[0])

            nc.vector.memset(eps[:], EPS).then_inc(eps_ok, 1)
            dve.wait_ge(iota_ok, 3)
            nc.vector.tensor_copy(hi_row[:], iot[:])
            nc.vector.tensor_copy(lo_row[:], iot[:, 0:P])
            nc.vector.tensor_scalar(lo1_row[:], iot[:, 0:P], 1.0, None, ALU.add)
            link(nc.vector.tensor_copy(pidx[:], pidx_i[:]))
            nc.vector.tensor_scalar(ident[:], lo_row[:], pidx[:, 0:1], None, ALU.is_equal)
            nc.vector.tensor_scalar(before[:], lo_row[:], pidx[:, 0:1], None, ALU.is_gt)
            nc.vector.tensor_scalar(notbefore[:], lo_row[:], pidx[:, 0:1], None, ALU.is_le)
            nc.vector.tensor_scalar(f_earlier[:], lo_row[:], pidx[:, 0:1], None, ALU.is_lt)
            nc.vector.tensor_copy(dump[:], dump_i[:]).then_inc(const_ok, 1)

            dve.wait_ge(src_in, 32)
            nc.vector.tensor_scalar(t1[:], srcI[:], 8, 0x3FFFFC, ALU.logical_shift_right, ALU.bitwise_and)
            nc.vector.tensor_scalar(t2[:], srcI[:], 3, None, ALU.bitwise_and)
            nc.vector.tensor_scalar(t3[:], srcI[:], 3, 127, ALU.logical_shift_right, ALU.bitwise_and)
            link(nc.vector.tensor_scalar(posI[:], srcI[:], 2, 1, ALU.logical_shift_right, ALU.bitwise_and))
            nc.vector.tensor_copy(loF[:], t3[:])
            nc.vector.tensor_tensor(hiF[:], t1[:], t2[:], ALU.add)
            nc.vector.tensor_copy(slot0[:], posI[:])
            link(nc.vector.tensor_copy(lo1F[:], t1[:]))
            link(nc.vector.tensor_scalar(lo1F[:], lo1F[:], NBF * HT - 0.5, None, ALU.is_gt))
            link(nc.vector.scalar_tensor_tensor(out=hiF[:], in0=lo1F[:], scalar=float(NBF * HT), in1=hiF[:], op0=ALU.mult, op1=ALU.add))
            link(nc.vector.scalar_tensor_tensor(out=hiF[:], in0=slot0[:], scalar=float(NBF * HT), in1=hiF[:], op0=ALU.mult, op1=ALU.add))
            link(nc.vector.tensor_tensor(lo1F[:], lo1F[:], slot0[:], ALU.mult))
            link(nc.vector.scalar_tensor_tensor(out=hiF[:], in0=lo1F[:], scalar=float(HT - NBF * HT), in1=hiF[:], op0=ALU.mult, op1=ALU.add))
            nc.vector.tensor_scalar(slot0[:].rearrange("p (a b) -> p a b", b=2)[:, :, 1],
                                    hiF[:].rearrange("p (a b) -> p a b", b=2)[:, :, 1], float(P // 2 * NT), None, ALU.add)
            nc.vector.tensor_copy(slot0[:].rearrange("p (a b) -> p a b", b=2)[:, :, 0],
                                  hiF[:].rearrange("p (a b) -> p a b", b=2)[:, :, 0])
            nc.vector.tensor_scalar(lo1F[:], loF[:], 1.0, None, ALU.add).then_inc(lo1_ok, 1)
            dve.wait_ge(lo1_ok, 1)

            dve.wait_ge(wT_done, 1)
            for k, dst in enumerate((W0aT, W0bT, W0cT)):
                nc.vector.tensor_copy(dst[:], ps[:, 0, k * P:(k + 1) * P])
            nc.vector.tensor_copy(vecs[:], ps[:, 1, P:P + 10]).then_inc(wT_ready, 1)
            dve.wait_ge(b0_done, 1)
            dve.wait_ge(wT_ready, 1)
            nc.vector.tensor_tensor(bias[:, 0:1], ps[:, 2, 0:1], vecs[:, 1:2], ALU.add).then_inc(bias_ok, 1)

            def onehot(t, i, p):
                wait(dve, cmp_done, t - 3)
                r = i % 4
                sc = (lambda a: a[0:p, t:t + 1]) if isinstance(t, int) else (lambda a: a[:, bass.ds(t, 1)])
                nc.vector.tensor_scalar(ohh[0:p, r, :], hi_row[0:p, :], sc(hiF), None, ALU.is_equal)
                nc.vector.tensor_scalar(ohl[0:p, r, :], lo_row[0:p, :], sc(loF), None, ALU.is_equal).then_inc(oh_ready, 1)

            def select(t, i, p, r_):
                dve.wait_ge(tri_done, t + 1)
                nc.vector.tensor_tensor_reduce(out=junk[0:p, i % 2, :], in0=ohh[0:p, i % 4, :], in1=ps[0:p, i % 2, 0:NT],
                                               scale=1.0, scalar=0.0, op0=ALU.mult, op1=ALU.add,
                                               accum_out=rank[0:p, r_ % 2, i:i + 1]).then_inc(rank_ready, 1)

            link(nc.vector.memset(rank[:], 0.0))
            onehot(0, 0, P)
            c0 = chain[0]

            def slots(b, r_, k):
                cols = slice(b * BI, (b + 1) * BI) if isinstance(b, int) else bass.ds(b * BI, BI)
                if k:
                    dve.wait_ge(dve_s, b * 3 + (c0 + k))
                if k == 0:
                    dve.wait_ge(rank_ready, (b + 1) * BI)
                    nc.vector.tensor_scalar(posf[:, 1, :], rank[:, r_ % 2, :], P // 2 - 0.5, None, ALU.is_gt)
                    nc.vector.scalar_tensor_tensor(out=posf[:, 0, :], in0=rank[:, r_ % 2, :], scalar=float(NT),
                                                   in1=slot0[:, cols], op0=ALU.mult, op1=ALU.add).then_inc(dve_s, 1)
                elif k == 1:
                    nc.vector.tensor_tensor(posf[:, 2, :], dump[:, cols], posf[:, 0, :], ALU.subtract).then_inc(dve_s, 1)
                elif k == 2:
                    nc.vector.tensor_tensor(posf[:, 2, :], posf[:, 2, :], posf[:, 1, :], ALU.mult).then_inc(dve_s, 1)
                else:
                    nc.vector.tensor_tensor(posI[:, cols], posf[:, 0, :], posf[:, 2, :], ALU.add).then_inc(pos_ready, 1)

            def rank_block(b, r_):
                p, pn = ep(b), ep(b + 1 if isinstance(b, int) else b)
                for i in range(BI):
                    t = b * BI + i
                    if not (isinstance(t, int) and t == NE - 1):
                        onehot(t + 1, (i + 1) % BI, pn if i == BI - 1 else p)
                    if i % 2 and not (isinstance(b, int) and b == 0):
                        slots(b - 1, (r_ - 1) % RING, i // 2)
                    select(t, i, p, r_)

            quads(dve, rank_block, 0, EB)
            for k in range(4):
                slots(EBF, EBF % RING, k)
            chain[0] = c0 + 3 * EB

            dve.wait_ge(cmp_done, NE)
            link(nc.vector.tensor_copy(tot[:], ps[:, 0, 0:NT]))
            link(nc.vector.tensor_tensor(tot[:], tot[:], ps[:, 1, 0:NT], ALU.max))
            link(nc.vector.tensor_reduce(tmax[:], tot[:], axis=AX, op=ALU.max))
            nc.vector.tensor_scalar(ovf[:], tmax[:], P // 2 + 0.5, None, ALU.is_gt).then_inc(ovf_ok, 1)
            link(nc.vector.tensor_scalar(rcnt[:], ps[:, 2, 0:NT], 1.0, None, ALU.max))
            nc.vector.reciprocal(rcnt[:], rcnt[:]).then_inc(rcnt_ok, 1)
            dve.wait_ge(rcnt_ok, 1)

            def merge(t, p):
                col = (lambda a: a[0:p, t:t + 1]) if isinstance(t, int) else (lambda a: a[:, bass.ds(t, 1)])

                def then(ins, k):
                    ins.then_inc(fch, 1)
                    dve.wait_ge(fch, t * 6 + k)

                wait(dve, f_done, 16 * t)
                key = f_key[0:p, 0:1]
                then(nc.vector.tensor_scalar(key, col(loF), float(NT), None, ALU.mult), 1)
                then(nc.vector.tensor_tensor(key, key, col(hiF), ALU.add), 2)
                nc.vector.tensor_copy(f_get[0:p, :], key)
                nc.vector.tensor_scalar(f_kb[0:p, :], lo1_row[0:p, :], 0.0, key, ALU.mult, ALU.add).then_inc(f_keys, 1)
                dve.wait_ge(f_row, t + 1)
                then(nc.vector.tensor_scalar(f_same[0:p, 0:p], ps[0:p, 6, 0:p], key, None, ALU.is_equal), 3)
                nc.vector.tensor_tensor(f_junk[0:p, 0:p], f_same[0:p, 0:p], f_earlier[0:p, 0:p], ALU.mult).then_inc(f_sameok, 1)
                dve.wait_ge(f_sameok, t + 1)
                then(nc.vector.tensor_reduce(f_key[0:p, 1:2], f_junk[0:p, 0:p], axis=AX, op=ALU.max), 4)
                then(nc.vector.tensor_scalar(f_key[0:p, 2:3], key, -1.0, dump[0:p, 0:1], ALU.mult, ALU.add), 5)
                then(nc.vector.tensor_tensor(f_key[0:p, 3:4], f_key[0:p, 1:2], f_key[0:p, 2:3], ALU.mult), 6)
                nc.vector.tensor_tensor(f_put[0:p, :], f_key[0:p, 3:4], key, ALU.add).then_inc(f_idx, 1)
                dve.wait_ge(f_got, 16 * (t + 1))
                dve.wait_ge(f_C, t + 1)
                nc.vector.tensor_scalar(f_new[0:p, D:RW], col(loF), 1.0, None, ALU.add)
                nc.vector.tensor_tensor(f_new[0:p, 0:D], ps[0:p, 7, 0:D], f_old[0:p, 0:D], ALU.add).then_inc(f_sum, 1)

            rebuild(dve, merge)

            def onehots(t, s):
                dve.wait_ge(tab_in[s], 16 * (t // PER + 1) if isinstance(t, int) else 4 * (t - s) + 16)
                wait(dve, mz_done, t - 1)
                pn = np_(t)
                lo1 = tabr[:, s, :].rearrange("p (i c) -> p i c", i=HT)[:, :, D:RW]
                nc.vector.tensor_tensor(oneh[:, s % 2, :].rearrange("p (i e) -> p i e", i=HT)[:, :, 0:pn],
                                        lo1_row[:, 0:pn].unsqueeze(1).to_broadcast([P, HT, pn]),
                                        lo1.to_broadcast([P, HT, pn]), ALU.is_equal).then_inc(oh0_ready, 1)

            def combine0(t, s):
                dve.wait_ge(mz_done, t + 1)
                dve.wait_ge(mx_ready, xnum(t) + 1)
                wait(dve, hT_done, t - 1)
                pn, q = np_(t), half_of(t, s)
                for j in range(HT):
                    c, i = slice(j * D, (j + 1) * D), q * HT + j
                    last = nc.vector.scalar_tensor_tensor(
                        out=total(s)[0:pn, c], in0=ps[0:pn, 4 + s % 2, c],
                        scalar=rcnt[0:pn, i:i + 1] if isinstance(q, int) else rcnt[:, bass.ds(i, 1)],
                        in1=part(t, s)[0:pn, c], op0=ALU.mult, op1=ALU.add)
                last.then_inc(sum_ready, 1)

            def stat(l, q, ready, n):
                dve.wait_ge(ready, n)
                dst = stats[:, q, :] if isinstance(q, int) else stats[:, bass.ds(q, 1), :].rearrange("p a c -> p (a c)")
                nc.vector.bn_stats(dst, hcol(q)).then_inc(stl[l], 1)

            def layer0(t, s):
                some = lambda k: not (isinstance(t, int) and (t < k or t - k >= NH))
                if some(-1):
                    onehots(t + 1, (s + 1) % PER)
                if some(1) and has_x(t - 1, s - 1):
                    combine0(t - 1, (s - 1) % PER)
                if some(4):
                    stat(0, half_of(t - 4, s), h0_ready, t - 3)

            dve.wait_ge(px_Mc, XH)
            onehots(0, 0)
            halves(dve, layer0)
            for t in range(NH, NH + 4):
                layer0(t, t % PER)

            def batchnorm(l):
                dve.wait_ge(stl[l], NH)
                link(nc.vector.bn_aggr(agg[:], stats[:].rearrange("p a c -> p (a c)")))
                nc.vector.tensor_scalar(bn_t[:], agg[:, 1:2], EPS, None, ALU.add).then_inc(agg_ok, 1)
                dve.wait_ge(std_ok, l + 1)
                link(nc.vector.reciprocal(bn_std[:], bn_std[:]))
                link(nc.vector.tensor_tensor(bn_a[:, l:l + 1], bn_std[:], vecs[:, 4 + 2 * l:5 + 2 * l], ALU.mult))
                link(nc.vector.tensor_tensor(bn_t[:], agg[:, 0:1], bn_a[:, l:l + 1], ALU.mult))
                nc.vector.tensor_tensor(bn_c[:, l:l + 1], vecs[:, 5 + 2 * l:6 + 2 * l], bn_t[:], ALU.subtract).then_inc(ac_ok, 1)

            dve.wait_ge(w12T_done, 1)
            nc.vector.tensor_copy(oneh[:, 0, 0:2 * P], ps[:, 0, 0:2 * P]).then_inc(w12_ok, 1)
            dve.wait_ge(w12_ok, 1)
            for l, W in ((1, W1T), (2, W2T)):
                batchnorm(l - 1)
                dve.wait_ge(bmm_ok, l)
                nc.vector.tensor_scalar(W, W, bn_a[:, l - 1:l], None, ALU.mult)
                nc.vector.tensor_tensor(bias[:, l:l + 1], ps[:, 7, 0:1], vecs[:, 1 + l:2 + l], ALU.add).then_inc(fold_ok, 1)
                halves(dve, lambda q, s: stat(l, q, hr[l], q + 1))
            batchnorm(2)

            def residual(q, s):
                dve.wait_ge(sum_done, q + 1)
                dve.wait_ge(x2_in[s % PER], 16 * (q // PER + 1) if isinstance(q, int) else 4 * (q - s % PER) + 16)
                z = zcol(q)[0:np_(q), :]
                nc.vector.tensor_tensor(z, ps[0:np_(q), s, :], z, ALU.add).then_inc(res_ready, 1)

            def stats_may(q, s):
                if dve_adds(s):
                    dve.wait_ge(res_ready, (q - 3) // PER + 1)
                else:
                    dve.wait_ge(sum_done, q + 1)
                wait(dve, lnm1_ok, pair(q - 2, s))

            def ln_stats(q, s):
                pn = np_(q)
                z = zcol(q) if dve_adds(s) else ps[:, s, :]
                for j in range(HT):
                    last = nc.vector.bn_stats(lnst[0:pn, s // 2 % 2, s % 2 * HT + j, :], z[0:pn, j * D:(j + 1) * D])
                last.then_inc(lnst_ok, 1)

            def rstd(q, s):
                dve.wait_ge(lnsd_ok, pair(q, s) + 1)
                pn, r = np_(q), s // 2
                nc.vector.reciprocal(lnm[0:pn, r, 3, :], lnm[0:pn, r, 2, :]).then_inc(lnrs_ok, 1)

            def ln_apply(q, s):
                dve.wait_ge(lnr_ok, pair(q, s) + 1)
                pn, r = np_(q), s // 2
                for j in range(HT):
                    c, i = slice(j * D, (j + 1) * D), s % 2 * HT + j
                    v = zcol(q)[0:pn, c]
                    last = nc.vector.tensor_scalar(v, v if dve_adds(s) else ps[0:pn, s, c], lnm[0:pn, r, 3, i:i + 1], lnm[0:pn, r, 4, i:i + 1], ALU.mult, ALU.add)
                last.then_inc(lnv_ready, 1)

            def final(q, s):
                some = lambda k: not (isinstance(q, int) and (q < k or q - k >= NH))
                if dve_adds(s) and some(0):
                    residual(q, s)
                if some(0):
                    stats_may(q, s)
                if s % 2 and some(4):
                    ln_apply(q - 4, (s - 4) % BANKS)
                if s % 2 == 0 and some(4):
                    rstd(q - 4, (s - 4) % BANKS)
                if some(0):
                    ln_stats(q, s)

            halves(dve, final, per=BANKS)
            for q in range(NH, NH + 4):
                final(q, q % BANKS)

        @block.tensor
        def _(pe):
            pe.wait_ge(const_ok, 1)
            pe.wait_ge(w_in, 16)
            pe.wait_ge(v_in, 160)
            for k in range(3):
                nc.tensor.transpose(ps[:, 0, k * P:(k + 1) * P], wraw[:, k, :], ident[:])
            nc.tensor.transpose(ps[:, 1, P:P + 10], vraw[:, :], ident[0:10, 0:10]).then_inc(wT_done, 1)
            pe.wait_ge(wT_ready, 1)
            nc.tensor.matmul(ps[:, 2, 0:1], W0cT[:], vecs[:, 0:1], start=True, stop=True).then_inc(b0_done, 1)
            pe.wait_ge(bias_ok, 1)

            def transpose_e(b, k, r_):
                hf = 2 * b + k
                p = ep(b)
                if k == 0:
                    n = b // RING + 1 if isinstance(b, int) else None
                    pe.wait_ge(e_in[r_], 16 * n if isinstance(b, int) else 4 * (b - r_) + 16)
                wait(pe, eT_ready, hf)
                for i in range(HT):
                    c = (k * HT + i) * D
                    last = nc.tensor.transpose(ps[:, 3, i * P:i * P + p], er[0:p, r_, c:c + D], ident[0:p, 0:p])
                last.then_inc(eT_done, 1)

            def project_e(b, k, tiles=range(HT)):
                hf = 2 * b + k
                p = ep(b)
                if 0 in tiles:
                    pe.wait_ge(eT_ready, hf + 1)
                    wait(pe, rows_ready, hf)
                for i in tiles:
                    last = nc.tensor.matmul(ps[0:p, 5, i * D:(i + 1) * D], stage[:, 0, i * P:i * P + p], W0bT[:],
                                            start=True, stop=True)
                if HT - 1 in tiles:
                    last.then_inc(pj_done, 1)

            def transpose_x(i, s):
                pe.wait_ge(px_in[s], 16 * (i // PER + 1) if isinstance(i, int) else 4 * (i - s) + 16)
                wait(pe, px_Tc, i - 1)
                for j in range(HT):
                    last = nc.tensor.transpose(ps[:, 4 + 3 * (s % 2), j * P:(j + 1) * P], xr[:, s, j * D:(j + 1) * D], ident[:])
                last.then_inc(px_T, 1)

            def project_x(i, s, tiles=range(HT)):
                if 0 in tiles:
                    pe.wait_ge(px_Tc, i + 1)
                    wait(pe, px_Mc, i)
                for j in tiles:
                    last = nc.tensor.matmul(ps[:, 6, j * D:(j + 1) * D], xT_places[s % 2][:, j * P:(j + 1) * P], W0aT[:],
                                            start=True, stop=True)
                if HT - 1 in tiles:
                    last.then_inc(px_M, 1)

            def rest(t, i, p):
                pe.wait_ge(rank_ready, t + 1)
                nc.tensor.matmul(ps[:, i % 2, 0:NT], notbefore[0:p, :], ohh[0:p, i % 4, :],
                                 start=False, stop=False, skip_group_check=True).then_inc(cmp_done, 1)

            def count(b, i):
                p, t = ep(b), b * BI + i
                first = isinstance(t, int) and t == 0
                pe.wait_ge(oh_ready, t + 1)
                nc.tensor.matmul(ps[0:p, i % 2, 0:NT], before[0:p, 0:p], ohh[0:p, i % 4, :],
                                 start=isinstance(t, int) and t < 2, stop=False, skip_group_check=True).then_inc(tri_done, 1)
                nc.tensor.matmul(ps[:, 2, 0:NT], ohl[0:p, i % 4, :], ohh[0:p, i % 4, :],
                                 start=first, stop=isinstance(t, int) and t == NE - 1, skip_group_check=True)
                if not first:
                    rest(t - 1, (i - 1) % BI, p if i else P)

            def early(b, r_):
                for i in range(BI):
                    count(b, i)

            def middle(b, r_):
                with_x = not (isinstance(b, int) and b == LAG)
                j, one, two = b - LAG, range(HT // 2), range(HT // 2, HT)
                for i in range(BI):
                    count(b, i)
                    if i == 0:
                        transpose_e(j, 0, r_)
                    if i == 1 and with_x:
                        transpose_x(j - 1, (r_ - 1) % PER)
                    if i == 2:
                        project_e(j, 0, one)
                    if i == 3:
                        project_e(j, 0, two)
                    if i == 4:
                        transpose_e(j, 1, r_)
                    if i == 5 and with_x:
                        project_x(j - 1, r_ - 1, one)
                    if i == 6:
                        if with_x:
                            project_x(j - 1, r_ - 1, two)
                        project_e(j, 1, one)
                    if i == 7:
                        project_e(j, 1, two)

            def late(b, r_, with_x=True):
                if isinstance(b, int) and b == EBF:
                    for i in range(BI):
                        count(b, i)
                if isinstance(b, int) and b == EB:
                    rest(NE - 1, BI - 1, EPL)
                before_x, xs = late_x(b, r_, -1), [late_x(b, r_, m) for m in range(LATE)]
                transpose_e(b - LAG, 0, r_)
                if not (isinstance(b, int) and b == EBF):
                    project_x(*before_x)
                transpose_x(*xs[0])
                project_e(b - LAG, 0)
                if with_x:
                    transpose_x(*xs[1])
                project_x(*xs[0])
                transpose_e(b - LAG, 1, r_)
                if with_x:
                    project_x(*xs[1])
                    transpose_x(*xs[2])
                project_e(b - LAG, 1)
                if with_x:
                    transpose_x(*xs[3])
                    project_x(*xs[2])

            quads(pe, early, 0, LAG)
            quads(pe, middle, LAG, EBF)
            quads(pe, late, EBF, EB + LAG - 1)
            late(EB + LAG - 1, (EB + LAG - 1) % RING, with_x=False)
            pe.wait_ge(rows_ready, 2 * EB)
            pe.wait_ge(px_Mc, XH)

            def xT(t, s):
                i = xplace(t, s)
                pe.wait_ge(x_in[i], 16 * (xnum(t) // 2 + 1) if isinstance(t, int) else 4 * (t - s) + 16)
                wait_x(pe, xT_ready, t)
                pn = np_(t)
                for j in range(HT):
                    last = nc.tensor.transpose(ps[:, i, j * P:j * P + pn], xr[0:pn, i, j * D:(j + 1) * D], ident[0:pn, 0:pn])
                last.then_inc(xT_done, 1)

            def mx(t, s):
                pe.wait_ge(xT_ready, xnum(t) + 1)
                wait_x(pe, mx_ready, t)
                pn, i = np_(t), xplace(t, s)
                for j in range(HT):
                    last = nc.tensor.matmul(ps[0:pn, 2 + i, j * D:(j + 1) * D], stage[:, i, j * P:j * P + pn], W0aT[:],
                                            start=True, stop=True)
                last.then_inc(mx_done, 1)

            def mz(t, s):
                pn = np_(t)
                if s % 2 == 0:
                    wait(pe, sum_ready, xnum(t))
                elif not (isinstance(t, int) and t < 2):
                    pe.wait_ge(zc_ready, (t - 1) // 2)
                pe.wait_ge(oh0_ready, t + 1)
                for j in range(HT):
                    last = nc.tensor.matmul(ps[0:pn, 4 + s % 2, j * D:(j + 1) * D], oneh[:, s % 2, j * P:j * P + pn],
                                            tabr[:, s, j * RW:j * RW + D], start=True, stop=True)
                last.then_inc(mz_done, 1)

            def hT(t, s):
                if has_x(t, s):
                    pe.wait_ge(sum_ready, xnum(t) + 1)
                else:
                    pe.wait_ge(sum2_ready, (t - 1) // 2 + 1)
                wait(pe, h0_ready, t - 1)
                pn = np_(t)
                for j in range(HT):
                    last = nc.tensor.transpose(ps[:, 6 + s % 2, j * pn:(j + 1) * pn], total(s)[0:pn, j * D:(j + 1) * D],
                                               ident[0:pn, 0:pn])
                last.then_inc(hT_done, 1)

            pe.wait_ge(rcnt_ok, 1)

            def sums(t, p):
                pe.wait_ge(f_in, 16 * (t + 1))
                nc.tensor.transpose(ps[:, 3, 0:p], f_e[0:p, :], ident[0:p, 0:p]).then_inc(f_T, 1)
                pe.wait_ge(f_Tc, t + 1)
                nc.tensor.matmul(ps[0:p, 5, 0:D], f_eT[:, 0:p], W0bT[:], start=True, stop=True).then_inc(f_P, 1)
                pe.wait_ge(f_keys, t + 1)
                nc.tensor.matmul(ps[0:p, 6, 0:p], f_kb[0:p, 0:p], ident[0:p, 0:p], start=True, stop=True).then_inc(f_row, 1)
                pe.wait_ge(f_Pc, t + 1)
                pe.wait_ge(f_idx, t + 1)
                nc.tensor.matmul(ps[0:p, 7, 0:D], f_same[0:p, 0:p], f_p[0:p, :], start=True, stop=True).then_inc(f_C, 1)

            rebuild(pe, sums)
            xT(0, 0)
            xT(2, 2)
            mx(0, 0)

            def layer0(t, s):
                some = lambda k: not (isinstance(t, int) and (t < k or t - k >= NH))
                if s % 2 and some(-1):
                    xT(x_after(t, 3), (s + 3) % PER)
                if s % 2 == 0 and some(-1):
                    mx(x_after(t, 2), (s + 2) % PER)
                if some(0):
                    mz(t, s)
                if some(2):
                    hT(t - 2, (s - 2) % PER)

            halves(pe, layer0)
            for t in range(NH, NH + 2):
                layer0(t, t % PER)

            pe.wait_ge(w12_in, 32)
            pe.wait_ge(xT_ready, NBF + 2)
            nc.tensor.transpose(ps[:, 0, 0:P], tabr[:, 0, 0:P], ident[:])
            nc.tensor.transpose(ps[:, 0, P:2 * P], tabr[:, 0, P:2 * P], ident[:]).then_inc(w12T_done, 1)
            pe.wait_ge(w12_ok, 1)

            for l, W in ((1, W1T), (2, W2T)):
                pe.wait_ge(ac_ok, l)
                nc.tensor.matmul(ps[:, 7, 0:1], W, bn_c[:, l - 1:l], start=True, stop=True).then_inc(bmm_ok, 1)
                pe.wait_ge(fold_ok, l)

                def layer(q, s):
                    wait(pe, hr[l], q - 3)
                    pn = np_(q)
                    nc.tensor.matmul(ps[:, s, 0:HT * pn], W, hcol(q), start=True, stop=True).then_inc(mm[l], 1)

                halves(pe, layer)

            pe.wait_ge(hr[2], NH)

            def total3(q, s):
                applied(pe, (q - BANKS, s % 2))
                pn = np_(q)
                if not dve_adds(s):
                    pe.wait_ge(x2_in[s % PER], 16 * (q // PER + 1) if isinstance(q, int) else 4 * (q - s % PER) + 16)
                    nc.tensor.matmul(ps[0:pn, s, :], ident[0:pn, 0:pn], zcol(q)[0:pn, :], start=True, stop=False,
                                     skip_group_check=True)
                pe.wait_ge(y_ready, q + 1)
                for j in range(HT):
                    y, dst = stage[:, s % 2, j * pn:(j + 1) * pn], ps[0:pn, s, j * P:(j + 1) * P]
                    if dve_adds(s):
                        last = nc.tensor.transpose(dst, y, ident[:])
                    else:
                        last = nc.tensor.matmul(dst, y, ident[:], start=False, stop=j == HT - 1, skip_group_check=True)
                last.then_inc(sum_done, 1)

            halves(pe, total3, per=BANKS)


_USED = ["x", "src", "edge_attr_128", "L0_gnn_u", "L0_gnn_W0", "L0_gnn_b0", "L0_gnn_W1", "L0_gnn_b1", "L0_gnn_W2", "L0_gnn_b2",
         "L0_gnn_g0", "L0_gnn_bt0", "L0_gnn_g1", "L0_gnn_bt1", "L0_gnn_g2", "L0_gnn_bt2"]


def kernel(**inputs):
    import numpy as _np
    import concourse.bacc as _bacc
    from concourse import mybir as _mybir
    from concourse.bass_utils import run_bass_kernel_spmd as _run

    nc = _bacc.Bacc("TRN2", target_bir_lowering=False, num_devices=1, dynamic_dma_scratch_size=2048)
    arrays, args = {}, []
    for name in _USED:
        a = _np.ascontiguousarray(inputs[name])
        arrays[f"in_{name}"] = a
        args.append(nc.dram_tensor(f"in_{name}", a.shape, _mybir.dt.from_np(a.dtype), kind="ExternalInput").ap())
    n = inputs["x"].shape[0]
    tiles = (n + 1023) // 1024 * 8
    table = nc.dram_tensor("edge_table", (128 * tiles + 128 * ((inputs["src"].shape[0] + 1023) // 1024 * 8), 129), _mybir.dt.float32, kind="Internal").ap()
    out = nc.dram_tensor("out", inputs["x"].shape, _mybir.dt.float32, kind="ExternalOutput").ap()
    gnn_resnorm_kernel(nc, *args, table, out)
    r = _run(nc, [arrays], core_ids=[0])
    return r.results[0]["out"]
```
